# Optimizing a Trainium2 kernel written in Bass

```python
import numpy as np
import jax
import jax.numpy as jnp

def _softmax(x, axis=-1):
    return jax.nn.softmax(x, axis=axis)

def _gelu(x):
    return jax.nn.gelu(x, approximate=True)

def _silu(x):
    return jax.nn.silu(x)

def _sigmoid(x):
    return jax.nn.sigmoid(x)

def _layernorm(x, axis=-1, eps=1e-05):
    m = jnp.mean(x, axis=axis, keepdims=True)
    v = jnp.var(x, axis=axis, keepdims=True)
    return (x - m) / jnp.sqrt(v + eps)

def _scatter_add(tgt, idx, src, axis=0):
    return tgt.at[idx].add(src)

def _segment_sum(src, seg, n):
    return jax.ops.segment_sum(src, seg, n)
kernel_name = 'mk_adaln_d1_jaxref_r8_2eb056'

def setup_inputs(seed: int=0):
    np.random.seed(seed)
    _w = jnp.asarray

    def _L0_attn_setup():
        import math
        import jax, jax.numpy as jnp
        import numpy as np
        D_MODEL = 128
        N_HEADS = 16
        D_K = D_MODEL // N_HEADS
        D_C = 32
        B, S = (2, 256)
        key = jax.random.key(seed)
        ks = jax.random.split(key, 7)
        sd = lambda fan_in: 1.0 / math.sqrt(fan_in)
        return {'x': jax.random.normal(ks[0], (B, S, D_MODEL), dtype=jnp.float32), 'W_dq': jax.random.uniform(ks[1], (D_MODEL, D_C), minval=-sd(D_MODEL), maxval=sd(D_MODEL), dtype=jnp.float32), 'W_uq': jax.random.uniform(ks[2], (D_C, N_HEADS * D_K), minval=-sd(D_C), maxval=sd(D_C), dtype=jnp.float32), 'W_dkv': jax.random.uniform(ks[3], (D_MODEL, D_C), minval=-sd(D_MODEL), maxval=sd(D_MODEL), dtype=jnp.float32), 'W_uk': jax.random.uniform(ks[4], (D_C, N_HEADS * D_K), minval=-sd(D_C), maxval=sd(D_C), dtype=jnp.float32), 'W_uv': jax.random.uniform(ks[5], (D_C, N_HEADS * D_K), minval=-sd(D_C), maxval=sd(D_C), dtype=jnp.float32), 'W_o': jax.random.uniform(ks[6], (N_HEADS * D_K, D_MODEL), minval=-sd(N_HEADS * D_K), maxval=sd(N_HEADS * D_K), dtype=jnp.float32)}
    _L0_attn_in = _L0_attn_setup()

    def _L0_ffn_setup():
        import jax, jax.numpy as jnp
        import numpy as np
        B, T, C = (2, 64, 128)
        I = 512
        E = 8
        K = 2
        key = jax.random.key(seed)
        ks = jax.random.split(key, 8)
        s = 0.02
        return {'x': jax.random.normal(ks[0], (B, T, C), jnp.float32), 'Wr1': jax.random.normal(ks[1], (C, C // 4), jnp.float32) * s, 'br1': jnp.zeros((C // 4,), jnp.float32), 'Wr2': jax.random.normal(ks[2], (C // 4, E), jnp.float32) * s, 'br2': jnp.zeros((E,), jnp.float32), 'Ws1': jax.random.normal(ks[3], (C, I), jnp.float32) * s, 'bs1': jnp.zeros((I,), jnp.float32), 'Ws2': jax.random.normal(ks[4], (I, C), jnp.float32) * s, 'bs2': jnp.zeros((C,), jnp.float32), 'We1': jax.random.normal(ks[5], (E, C, I), jnp.float32) * s, 'be1': jnp.zeros((E, I), jnp.float32), 'We2': jax.random.normal(ks[6], (E, I, C), jnp.float32) * s, 'be2': jnp.zeros((E, C), jnp.float32)}
    _L0_ffn_in = _L0_ffn_setup()
    _L0_c = _w((lambda *s: np.random.randn(*s).astype(np.float32) * 0.05)(2, 128))
    _L0_wmod = _w((lambda *s: np.random.randn(*s).astype(np.float32) * 0.05)(128, 6 * 128) * 128 ** (-0.5))
    _d = {'L0_attn_x': _L0_attn_in['x'], 'L0_attn_W_dq': _L0_attn_in['W_dq'], 'L0_attn_W_uq': _L0_attn_in['W_uq'], 'L0_attn_W_dkv': _L0_attn_in['W_dkv'], 'L0_attn_W_uk': _L0_attn_in['W_uk'], 'L0_attn_W_uv': _L0_attn_in['W_uv'], 'L0_attn_W_o': _L0_attn_in['W_o'], 'L0_ffn_Wr1': _L0_ffn_in['Wr1'], 'L0_ffn_br1': _L0_ffn_in['br1'], 'L0_ffn_Wr2': _L0_ffn_in['Wr2'], 'L0_ffn_br2': _L0_ffn_in['br2'], 'L0_ffn_Ws1': _L0_ffn_in['Ws1'], 'L0_ffn_bs1': _L0_ffn_in['bs1'], 'L0_ffn_Ws2': _L0_ffn_in['Ws2'], 'L0_ffn_bs2': _L0_ffn_in['bs2'], 'L0_ffn_We1': _L0_ffn_in['We1'], 'L0_ffn_be1': _L0_ffn_in['be1'], 'L0_ffn_We2': _L0_ffn_in['We2'], 'L0_ffn_be2': _L0_ffn_in['be2'], 'L0_c': _L0_c, 'L0_wmod': _L0_wmod}
    _x0 = _d['L0_attn_x']
    _d['L0_attn_x'] = jax.random.normal(jax.random.fold_in(jax.random.key(seed), 1), (2, 1024, 128), dtype=_x0.dtype)
    del _x0
    return _d

def reference(L0_attn_x, L0_attn_W_dq, L0_attn_W_uq, L0_attn_W_dkv, L0_attn_W_uk, L0_attn_W_uv, L0_attn_W_o, L0_ffn_Wr1, L0_ffn_br1, L0_ffn_Wr2, L0_ffn_br2, L0_ffn_Ws1, L0_ffn_bs1, L0_ffn_Ws2, L0_ffn_bs2, L0_ffn_We1, L0_ffn_be1, L0_ffn_We2, L0_ffn_be2, L0_c, L0_wmod):

    def _L0_attn_ref(x, W_dq, W_uq, W_dkv, W_uk, W_uv, W_o):
        import math
        import jax, jax.numpy as jnp
        import numpy as np
        D_MODEL = 128
        N_HEADS = 16
        D_K = D_MODEL // N_HEADS
        D_C = 32
        B, S = (2, 256)
        Bx, Sx, _ = x.shape
        c_q = x @ W_dq
        Q = (c_q @ W_uq).reshape(Bx, Sx, N_HEADS, D_K)
        c_kv = x @ W_dkv
        K = (c_kv @ W_uk).reshape(Bx, Sx, N_HEADS, D_K)
        V = (c_kv @ W_uv).reshape(Bx, Sx, N_HEADS, D_K)
        scores = jnp.einsum('bqhd,bkhd->bhqk', Q, K) / math.sqrt(D_K)
        causal = jnp.tril(jnp.ones((Sx, Sx), dtype=bool))
        scores = jnp.where(causal, scores, -jnp.inf)
        attn = jax.nn.softmax(scores, axis=-1)
        out = jnp.einsum('bhqk,bkhd->bqhd', attn, V).reshape(Bx, Sx, N_HEADS * D_K)
        return out @ W_o

    def _L0_ffn_ref(x, Wr1, br1, Wr2, br2, Ws1, bs1, Ws2, bs2, We1, be1, We2, be2):
        import jax, jax.numpy as jnp
        import numpy as np
        B, T, C = (2, 64, 128)
        I = 512
        E = 8
        K = 2
        Bb, Tt, Cc = x.shape
        xf = x.reshape(-1, Cc)
        logits = jax.nn.relu(xf @ Wr1 + br1) @ Wr2 + br2
        gates = jax.nn.softmax(logits, axis=-1)
        tg, ti = jax.lax.top_k(gates, K)
        tg = jax.nn.softmax(tg / K, axis=-1)
        out = jax.nn.silu(xf @ Ws1 + bs1) @ Ws2 + bs2
        for e in range(E):
            h = jax.nn.silu(xf @ We1[e] + be1[e]) @ We2[e] + be2[e]
            w = jnp.sum(tg * (ti == e), axis=-1)
            out = out + w[:, None] * h
        return out.reshape(Bb, Tt, Cc)
    x = L0_attn_x
    mod = (_silu(L0_c) @ L0_wmod).reshape(L0_c.shape[0], 6, 1, -1)
    sa, ca, ga, sb, cb, gb = (mod[:, 0], mod[:, 1], mod[:, 2], mod[:, 3], mod[:, 4], mod[:, 5])
    ga = (2 * (ga >= 0) - 1) * jnp.maximum(jnp.abs(ga), 0.25)
    gb = (2 * (gb >= 0) - 1) * jnp.maximum(jnp.abs(gb), 0.25)
    h = _layernorm(x, axis=-1) * (1 + ca) + sa
    x = x + ga * _L0_attn_ref(h, L0_attn_W_dq, L0_attn_W_uq, L0_attn_W_dkv, L0_attn_W_uk, L0_attn_W_uv, L0_attn_W_o)
    h = _layernorm(x, axis=-1) * (1 + cb) + sb
    x = x + gb * _L0_ffn_ref(h, L0_ffn_Wr1, L0_ffn_br1, L0_ffn_Wr2, L0_ffn_br2, L0_ffn_Ws1, L0_ffn_bs1, L0_ffn_Ws2, L0_ffn_bs2, L0_ffn_We1, L0_ffn_be1, L0_ffn_We2, L0_ffn_be2)
    return x

_drawn_inputs = setup_inputs


def setup_inputs(seed=0):
    import zlib

    import numpy as np

    out = dict(_drawn_inputs(seed))
    spreads = {'L0_ffn_br1': (0.0, 2.0),
     'L0_ffn_br2': (0.0, 2.0),
     'L0_ffn_bs1': (0.0, 2.0),
     'L0_ffn_bs2': (0.0, 2.0),
     'L0_ffn_be1': (0.0, 2.0),
     'L0_ffn_be2': (0.0, 2.0)}
    factors = {'L0_attn_W_dq': 8.0,
     'L0_attn_W_uq': 8.0,
     'L0_attn_W_dkv': 8.0,
     'L0_attn_W_uk': 8.0,
     'L0_attn_W_uv': 8.0,
     'L0_attn_W_o': 8.0,
     'L0_ffn_Wr1': 31.125,
     'L0_ffn_Wr2': 15.67,
     'L0_ffn_Ws1': 26.184,
     'L0_ffn_Ws2': 17.798,
     'L0_ffn_We1': 25.163,
     'L0_ffn_We2': 18.665}
    for name, (base, spread) in spreads.items():
        noise = np.random.default_rng([zlib.crc32(name.encode()), seed]).standard_normal(out[name].shape)
        drawn = base * np.exp(spread * noise) if base else spread * noise
        out[name] = jnp.asarray(drawn.astype(out[name].dtype))
    for name, factor in factors.items():
        out[name] = (out[name] * factor).astype(out[name].dtype)
    return out
```

```python
from contextlib import ExitStack

import concourse.bass as bass
from concourse import mybir

ALU = mybir.AluOpType
ACT = mybir.ActivationFunctionType
AX_X = mybir.AxisListType.X
F32 = mybir.dt.float32
BF16 = mybir.dt.bfloat16
U32 = mybir.dt.uint32

P = 128
LOWEST = -3.0e38
EPS = 1e-5

SLOTS = [0, 7, 1, 6, 2, 5, 3, 4]
HQ = 4
DK = 8
VW = 32
NEG_ROW = 96
CROSS = 72


def score_units():
    out = []
    for j in SLOTS:
        w = 1024 - P * j
        n = 1 if w > 512 else (2 if w > 256 else 4)
        pitch = 1024 // n if w > 256 or n == 1 else w
        out.append([(j, h, n, w, pitch) for h in range(0, HQ, n)])
    return out


def max_units():
    out = []
    for i in range(8):
        w = P * (i + 1)
        if w > 512:
            out += [(i, 0, 512, False, 0), (i, 512, w - 512, True, 1)]
        else:
            out.append((i, 0, w, True, 0))
    return out


def adaln_layer(nc, x, cT, wmod, wdqT, wdkvT, wuq, wuk, wuv, wo, wr1, br1, wr2, br2,
                ws1, ws2, bs2, we1, we2, be2, b1T, out):
    B, S, C = x.shape
    assert (B, S, C) == (2, 1024, 128)
    NT = B * S // P
    NE = we1.shape[0]
    FF = ws1.shape[1]
    NF = FF // P
    NQ = 16 // HQ
    T = B * NQ
    UNITS = score_units()
    NU = sum(len(u) for u in UNITS)
    UBASE = [sum(len(u) for u in UNITS[:s]) for s in range(9)]
    MAXU = [(h, *m) for h in range(HQ) for m in max_units()]
    NM = len(MAXU)
    AUX0 = NM + 1
    AUXN = NM + 3
    NLOAD = 12
    STEPS = 4

    with ExitStack() as ctx:
        def sb(name, shape, dt):
            return ctx.enter_context(nc.sbuf_tensor(name, shape, dt))

        def sem(name):
            return ctx.enter_context(nc.semaphore(name))

        sc = ctx.enter_context(nc.psum_tensor("sc", [P, 4, 512], F32))
        aux = ctx.enter_context(nc.psum_tensor("aux", [P, 2, 512], F32))
        oacc = ctx.enter_context(nc.psum_tensor("oacc", [P, 2, 512], F32))

        x_sb = sb("x_sb", [P, NT, C], F32)
        cT_sb = sb("cT_sb", [P, B], F32)
        cs = sb("cs", [P, B], F32)
        csB = sb("csB", [P, B, P], F32)
        wmod_sb = sb("wmod_sb", [P, 6 * C], F32)
        wd_sb = sb("wd_sb", [32, 2, C], F32)
        wu_sb = sb("wu_sb", [32, 3, C], F32)
        wo_sb = sb("wo_sb", [P, C], F32)
        wr1_sb = sb("wr1_sb", [P, 32], F32)
        br1_sb = sb("br1_sb", [32, 1], F32)
        wr2_sb = sb("wr2_sb", [33, NE], F32)
        be2_sb = sb("be2_sb", [NE + 1, C], F32)
        b1_sb = sb("b1_sb", [P, (NE + 1) * NF], F32)
        ident = sb("ident", [P, P], F32)
        identb = sb("identb", [P, P], BF16)
        after = sb("after", [P, P], BF16)
        slab = sb("slab", [P, 512], F32)
        iota8 = sb("iota8", [P, NE], F32)
        wqkv = sb("wqkv", [P, 3, C], F32)
        modT = sb("modT", [P, 6, B], F32)
        scl = sb("scl", [P, 2, B], F32)
        gB = sb("gB", [P, 2, B, C], F32)
        gabs = sb("gabs", [P, 2, B, C], F32)
        gsgn = sb("gsgn", [P, 2, B, C], F32)
        wog = sb("wog", [P, B, C], F32)
        stats = sb("stats", [P, NT, 6], F32)
        mv = sb("mv", [P, NT, 2], F32)
        var = sb("var", [P, NT], F32)
        std = sb("std", [P, NT], F32)
        rst = sb("rst", [P, NT], F32)
        nwt = sb("nwt", [P, NT], F32)
        hT = sb("hT", [P, NT * P], F32)
        parts = sb("parts", [P, 2, 3, NT * P], BF16)
        r1 = sb("r1", [P, 2, 512], F32)
        valt = sb("valt", [P, NT, C], F32)
        S1 = sb("S1", [P, 2, 2, HQ * S], BF16)
        S2 = sb("S2", [P, 2, 2, HQ * S], BF16)
        vb = sb("vb", [P, 2, 8, HQ, VW], F32)
        pr = sb("pr", [P, 2, HQ, S], F32)
        mxp = sb("mxp", [P, 2, HQ * 8, 2], F32)
        negm = sb("negm", [P, HQ * 8], F32)
        negr = sb("negr", [P, HQ * 8], F32)
        neg3 = sb("neg3", [P, 3, HQ * 8], BF16)
        negT = sb("negT", [96, P], BF16)
        osb = sb("osb", [P, 2, 512], F32)
        rden = sb("rden", [P, 2, 4, HQ], F32)
        attn = sb("attn", [P, NT, C], F32)
        xn = attn
        aT = S1[:, 0, :, :].rearrange("p a n -> p (a n)").bitcast(F32)[:, 0:1024].rearrange("p (a n) -> p a n", a=2)
        sT = pr
        wup = S2[:, 0, 0, :].bitcast(F32)[:, 0:2 * FF].rearrange("p (a n) -> p a n", a=2)
        wdn = S2[:, 0, 1, :].bitcast(F32)[:, 0:2 * FF].rearrange("p (a f c) -> p a f c", a=2, f=NF)
        acc = S2[:, 1, 0, :].bitcast(F32).rearrange("p (n c) -> p n c", c=C)
        yout = S2[:, 1, 1, :].bitcast(F32).rearrange("p (n c) -> p n c", c=C)
        h2T = hT
        r1T = sb("r1T", [33, NT * P], F32)
        lg = sb("lg", [P, NT, NE], F32)
        gt = sb("gt", [P, NT, NE], F32)
        gmx = sb("gmx", [P, NT], F32)
        gsm = sb("gsm", [P, NT], F32)
        top = sb("top", [P, NT, 8], F32)
        topi = sb("topi", [P, NT, 8], U32)
        topf = sb("topf", [P, NT, 2], F32)
        tw = sb("tw", [P, NT, 2], F32)
        wgt = sb("wgt", [P, NT, NE + 1], F32)
        wsel = sb("wsel", [P, NT, NE], F32)
        wT = S1[0:NE + 1, 1, 0, :].bitcast(F32)
        wcur = sb("wcur", [P, 2, NT], F32)
        bcur = sb("bcur", [P, 2, NF], F32)
        sh_up = sb("sh_up", [P, FF], F32)
        sh_dn = sb("sh_dn", [P, NF, C], F32)

        kd = nc.dram_tensor("k_parts", [T, HQ, 3, DK, S], BF16, kind="Internal").ap()
        qd = nc.dram_tensor("q_parts", [T, HQ, 3, DK, S], BF16, kind="Internal").ap()

        names = """x_in0 x_in1 w_in w2_in parts_out0 parts_out1 s1_in0 s1_in1 s2_in0 s2_in1 negrow y_out ew0 ew1
            const_ready pad_ready chain_v chain_p chain_a cs_ready csb_ready comp_ready wqkv_ready mod_ready mod_done
            var_ready std_ready xn_ready xT_ready hT_ready qk_ready hi_ready r1_ready mid_ready lo_ready
            v_ready v_done aux_ready aux_free negm_ready neg3_ready score_ready exp_done
            vb_ready pv_done o_done at_ready at_done pj_ready x2_done var2_ready std2_ready
            xn2_ready x2T_ready h2T_ready rt_ready r1T_ready lg_ready ge_ready gx_ready gp_ready wgt_ready wt_ready
            wT_ready up_ready silu_done dn_ready acc_done cur_ready y_ready wog_ready
            passed_v passed_s passed_p""".split()
        s = {n: sem(n) for n in names}
        x_in = [s["x_in0"], s["x_in1"]]
        parts_out = [s["parts_out0"], s["parts_out1"]]
        s1_in = [s["s1_in0"], s["s1_in1"]]
        s2_in = [s["s2_in0"], s["s2_in1"]]
        ew = [s["ew0"], s["ew1"]]

        block = ctx.enter_context(nc.Block())

        QK = [(b, kq, half) for b in range(B) for kq in range(2) for half in range(2)]
        qk_bank = [sc[:, 2, :], sc[:, 3, :], oacc[:, 1, :]]

        @block.sync
        def _(sp):
            xv = x.rearrange("b (n p) c -> b p n c", p=P)
            sp.dma_start(x_sb[:, 0:8, :], xv[0]).then_inc(x_in[0], 16)
            sp.dma_start(x_sb[:, 8:16, :], xv[1]).then_inc(x_in[1], 16)
            for dst, src in ((wr1_sb[:, :], wr1), (br1_sb[:, :], br1), (wr2_sb[0:32, :], wr2),
                             (wr2_sb[32:33, :], br2), (be2_sb[0:NE, :], be2), (be2_sb[NE:NE + 1, :], bs2),
                             (b1_sb[:, :], b1T), (sh_up[:, :], ws1),
                             (sh_dn[:, :, :], ws2.rearrange("(f p) c -> p f c", p=P))):
                sp.dma_start(dst, src).then_inc(s["w2_in"], 16)

            def store_parts(b):
                for kq, dst in ((0, kd), (1, qd)):
                    for part in range(3):
                        done = 4 * b + 2 * kq + 2
                        sp.wait_ge((s["hi_ready"], s["mid_ready"], s["lo_ready"])[part], done)
                        sp.dma_start(
                            dst[NQ * b:NQ * b + NQ, :, part, :, :].rearrange("t h d n -> (t h) d n"),
                            parts[:, kq, part, b * S:(b + 1) * S]).then_inc(parts_out[b], 16)

            def load_s1(u, p):
                sp.wait_ge(parts_out[p], 96)
                sp.sem_inc(s["passed_s"], 1)
                kt = kd[bass.ds(NQ * p + u, 1)].rearrange("t h a d n -> (t h) a d n")
                qt = qd[bass.ds(NQ * p + u, 1)].rearrange("t h a d n -> (t h) a d n")
                for a in range(3):
                    sp.dma_start(S1[24 * a:24 * a + 24, p, 0, :].rearrange("r (h n) -> r h n", h=HQ),
                                 kt.rearrange("h b d n -> (b d) h n")).then_inc(s1_in[p], 16)
                    for b in range(3):
                        r = 24 * a + 8 * b
                        sp.dma_start(S1[r:r + 8, p, 1, :].rearrange("r (h n) -> r h n", h=HQ),
                                     qt[:, a, :, :].rearrange("h d n -> d h n")).then_inc(s1_in[p], 16)

            def copy_s2(p):
                for kq in range(2):
                    sp.dma_start(S2[0:CROSS, p, kq, :], S1[0:CROSS, p, kq, :]).then_inc(s2_in[p], 16)

            def neg_rows(p):
                sp.dma_start(S2[NEG_ROW:NEG_ROW + 3, p, 1, :].rearrange("r (s q) -> r s q", q=P),
                             negT[:, :]).then_inc(s["negrow"], 16)

            store_parts(0)
            load_s1(0, 0)
            sp.wait_ge(s1_in[0], 16 * NLOAD)
            sp.wait_ge(s["pad_ready"], 1)
            copy_s2(0)
            store_parts(1)
            load_s1(0, 1)
            sp.wait_ge(s["aux_free"], AUX0)
            neg_rows(0)

            def body(t, u, p, load, more):
                if load:
                    sp.wait_ge(s["aux_ready"], AUX0 + AUXN * t - 1)
                    sp.wait_ge(s2_in[p], 32 * u + 32)
                    load_s1(u + 1, p)
                if more:
                    sp.wait_ge(s1_in[1 - p], 16 * NLOAD * (u + p + 1))
                    sp.sem_inc(s["passed_s"], 1)
                    sp.wait_ge(s["score_ready"], NU * t + UBASE[1])
                    copy_s2(1 - p)
                    sp.wait_ge(s["aux_free"], AUX0 + AUXN * t + NM + 1)
                    neg_rows(1 - p)

            with sp.Fori(0, T // 2 - 1) as u:
                for p in range(2):
                    body(2 * u + p, u, p, True, True)
            body(T - 2, T // 2 - 1, 0, False, True)

            sp.wait_ge(s["score_ready"], NU * T)
            with sp.Fori(0, NE // 2) as u:
                for p in range(2):
                    e = 2 * u + p
                    sp.wait_ge(s["dn_ready"], STEPS * e + 1)
                    sp.sem_inc(s["passed_s"], 1)
                    sp.dma_start(wup[:, p:p + 1, :],
                                 we1[bass.ds(e, 1)].rearrange("e c f -> c e f")).then_inc(ew[p], 16)
                    sp.dma_start(wdn[:, p, :, :],
                                 we2[bass.ds(e, 1)].rearrange("e (f p) c -> p (e f) c", p=P)).then_inc(ew[p], 16)
            yv = out.rearrange("b (n p) c -> p (b n) c", p=P)
            for g in range(4):
                sp.wait_ge(s["y_ready"], g + 1)
                sp.dma_start(yv[:, 4 * g:4 * g + 4, :], yout[:, 4 * g:4 * g + 4, :]).then_inc(s["y_out"], 16)
            sp.wait_ge(s["y_out"], 64)

        @block.gpsimd
        def _(pool):
            link = [0]

            def chained(ins):
                link[0] += 1
                ins.then_inc(s["chain_p"], 1)
                pool.wait_ge(s["chain_p"], link[0])

            chained(pool.memset(ident[:, :], 0.0))
            chained(pool.affine_select(out=ident[:, :], in_=ident[:, :], compare_op=ALU.not_equal, fill=1.0,
                                       base=0, pattern=[[-1, P]], channel_multiplier=1))
            pool.tensor_copy(identb[:, :], ident[:, :]).then_inc(s["const_ready"], 1)
            chained(pool.memset(after[:, :], 0.0))
            pool.affine_select(out=after[:, :], in_=after[:, :], compare_op=ALU.is_ge, fill=LOWEST,
                               base=0, pattern=[[1, P]], channel_multiplier=-1).then_inc(s["const_ready"], 1)
            chained(pool.memset(slab[:, :], 0.0))
            pool.affine_select(out=slab[:, 384:512], in_=slab[:, 384:512], compare_op=ALU.is_ge, fill=LOWEST,
                               base=0, pattern=[[-1, P]], channel_multiplier=1).then_inc(s["const_ready"], 1)
            pool.memset(mxp[:, :, :, :], LOWEST).then_inc(s["const_ready"], 1)
            pool.iota(iota8[:, :], pattern=[[1, NE]], base=0, channel_multiplier=0,
                      allow_small_or_imprecise_dtypes=True).then_inc(s["const_ready"], 1)
            pool.wait_ge(s["const_ready"], 5)
            for p in range(2):
                chained(pool.memset(S2[64:128, p, :, :].bitcast(F32), 0.0))
                chained(pool.memset(S2[NEG_ROW:NEG_ROW + 3, p, 0, :], 1.0))
            pool.memset(r1T[32:33, :], 1.0).then_inc(s["pad_ready"], 1)
            pool.wait_ge(s["pad_ready"], 1)
            for n, (b, kq, half) in enumerate(QK):
                cols = slice(b * S + 512 * half, b * S + 512 * half + 512)
                pool.wait_ge(s["mid_ready"], n + 1)
                pool.tensor_tensor(parts[:, kq, 2, cols], r1[:, n % 2, :], parts[:, kq, 1, cols],
                                   ALU.subtract).then_inc(s["lo_ready"], 1)
                if n == 3:
                    chained(pool.memset(vb[:, :, :, :, :], 0.0))
                    chained(pool.memset(vb[:, :, :, :, DK:DK + 1], 1.0))
            chained(pool.memset(wgt[:, :, NE:NE + 1], 1.0))

            def split_max(v):
                pool.sem_inc(s["passed_p"], 1)
                pool.tensor_copy(neg3[:, 0, :], negm[:, :]).then_inc(s["chain_p"], 1)
                pool.wait_ge(s["chain_p"], v + 1)
                pool.tensor_tensor(negr[:, :], negm[:, :], neg3[:, 0, :], ALU.subtract).then_inc(s["chain_p"], 1)
                pool.wait_ge(s["chain_p"], v + 2)
                pool.sem_inc(s["passed_p"], 1)
                pool.tensor_copy(neg3[:, 1, :], negr[:, :]).then_inc(s["chain_p"], 1)
                pool.wait_ge(s["chain_p"], v + 3)
                pool.tensor_tensor(neg3[:, 2, :], negr[:, :], neg3[:, 1, :], ALU.subtract).then_inc(s["neg3_ready"], 1)

            def values(u, p):
                pool.wait_ge(s["v_done"], 4)
                src = valt[:, 8 * p:8 * p + 8, bass.ds(HQ * DK * u, HQ * DK)]
                pool.tensor_copy(vb[:, p, :, :, 0:DK],
                                 src.rearrange("p j (h d) -> p j h d", h=HQ)).then_inc(s["vb_ready"], 1)

            base = link[0]
            values(0, 0)
            pool.wait_ge(s["negm_ready"], 1)
            split_max(base)

            def body(t, u, p):
                pool.wait_ge(s["pv_done"], 8 * t + 1)
                values(u + p, 1 - p)
                pool.wait_ge(s["negm_ready"], t + 2)
                split_max(base + 3 * t + 3)

            with pool.Fori(0, T // 2 - 1) as u:
                for p in range(2):
                    body(2 * u + p, u, p)
            body(T - 2, T // 2 - 1, 0)

            pool.wait_ge(s["wgt_ready"], 1)
            pool.wait_ge(s["w2_in"], 16 * 9)
            with pool.Fori(0, NE // 2) as u:
                for p in range(2):
                    e = 2 * u + p
                    pool.wait_ge(s["acc_done"], STEPS * e + 1)
                    pool.wait_ge(s["silu_done"], NF * STEPS * e + 1)
                    pool.tensor_copy(wcur[:, p, :], wgt[:, :, bass.ds(e, 1)].rearrange("p n e -> p (n e)"))
                    pool.tensor_copy(bcur[:, p, :], b1_sb[:, bass.ds(NF * e, NF)]).then_inc(s["cur_ready"], 1)

        @block.scalar
        def _(act):
            act.sem_inc(s["o_done"], 1)
            for dst, src in ((cT_sb[:, :], cT), (wmod_sb[:, :], wmod), (wd_sb[:, 0, :], wdqT), (wd_sb[:, 1, :], wdkvT),
                             (wu_sb[:, 0, :], wuq), (wu_sb[:, 1, :], wuk), (wu_sb[:, 2, :], wuv), (wo_sb[:, :], wo)):
                act.dma_start(dst, src).then_inc(s["w_in"], 16)
            act.wait_ge(s["w_in"], 128)
            act.activation(cs[:, :], cT_sb[:, :], ACT.Silu).then_inc(s["cs_ready"], 1)

            def root(b):
                act.wait_ge(s["var_ready"], b + 1)
                act.activation(std[:, 8 * b:8 * b + 8], var[:, 8 * b:8 * b + 8], ACT.Sqrt).then_inc(s["std_ready"], 1)

            def h_out(g):
                act.wait_ge(s["xT_ready"], g + 1)
                if g == 0:
                    act.wait_ge(s["mod_done"], 1)
                act.activation(hT[:, 512 * g:512 * g + 512], sc[:, g % 2, :], ACT.Identity,
                               bias=modT[:, 0, g // 2:g // 2 + 1],
                               scale=scl[:, 0, g // 2:g // 2 + 1]).then_inc(s["hT_ready"], 1)

            def hi(n):
                b, kq, half = QK[n]
                act.wait_ge(s["qk_ready"], n + 1)
                act.activation(parts[:, kq, 0, b * S + 512 * half:b * S + 512 * half + 512], qk_bank[n % 3],
                               ACT.Copy).then_inc(s["hi_ready"], 1)

            def mid(n):
                b, kq, half = QK[n]
                act.wait_ge(s["r1_ready"], n + 1)
                act.activation(parts[:, kq, 1, b * S + 512 * half:b * S + 512 * half + 512], r1[:, n % 2, :],
                               ACT.Copy).then_inc(s["mid_ready"], 1)

            def v_out(g):
                act.wait_ge(s["v_ready"], g + 1)
                act.activation(
                    valt[:, 4 * g:4 * g + 4, :], aux[:, g % 2, :].rearrange("p (n c) -> p n c", n=4),
                    ACT.Copy).then_inc(s["v_done"], 1)

            for b in range(B):
                root(b)
                h_out(2 * b)
                h_out(2 * b + 1)
                for k in range(4):
                    hi(4 * b + k)
                    if k:
                        mid(4 * b + k - 1)
                mid(4 * b + 3)
                v_out(2 * b)
                v_out(2 * b + 1)

            def exps(t, slot):
                for n, (j, h, nh, w, pitch) in enumerate(UNITS[slot]):
                    g = NU * t + UBASE[slot] + n
                    act.wait_ge(s["score_ready"], g + 1)
                    if n == 0:
                        if not isinstance(t, int) or 8 * t + slot > 1:
                            act.wait_ge(s["pv_done"], 8 * t + slot)
                    buf = (UBASE[slot] + n) % 2
                    src = sc[:, 2 * buf:2 * buf + 2, :].rearrange("p a c -> p (a c)")
                    src = src[:, 0:nh * pitch].rearrange("p (h c) -> p h c", h=nh)[:, :, 0:w]
                    act.activation(pr[:, slot % 2, h:h + nh, P * j:P * j + w], src, ACT.Exp,
                                   scale=float(DK) ** -0.5).then_inc(s["exp_done"], 1)

            def o_out(t, c, aux_before):
                act.wait_ge(s["pv_done"], 8 * t + 8 + c)
                if c == 0:
                    act.wait_ge(s["aux_ready"], aux_before)
                act.activation(osb[:, c, :], oacc[:, c, :], ACT.Copy).then_inc(s["o_done"], 1)

            exps(0, 0)

            def body(t, more):
                for slot in range(1, 8):
                    exps(t, slot)
                o_out(t, 0, AUX0 + AUXN * t)
                o_out(t, 1, None)
                if more:
                    exps(t + 1, 0)

            with act.Fori(0, T // 2 - 1) as u:
                for p in range(2):
                    body(2 * u + p, True)
            body(T - 2, True)
            body(T - 1, False)

            for g in range(4):
                act.wait_ge(s["at_ready"], g + 1)
                if g >= 2:
                    act.wait_ge(s["pj_ready"], g - 1)
                act.activation(aT[:, g % 2, :], sc[:, g, :], ACT.Copy).then_inc(s["at_done"], 1)
            act.wait_ge(s["var2_ready"], 1)
            act.activation(std[:, :], var[:, :], ACT.Sqrt).then_inc(s["std2_ready"], 1)
            for g in range(4):
                act.wait_ge(s["x2T_ready"], g + 1)
                act.activation(h2T[:, 512 * g:512 * g + 512], sc[:, g, :], ACT.Identity,
                               bias=modT[:, 3, g // 2:g // 2 + 1],
                               scale=scl[:, 1, g // 2:g // 2 + 1]).then_inc(s["h2T_ready"], 1)
                act.wait_ge(s["rt_ready"], g + 1)
                act.activation(r1T[0:32, 512 * g:512 * g + 512], aux[0:32, g % 2, :], ACT.Relu,
                               bias=br1_sb[:, 0:1]).then_inc(s["r1T_ready"], 1)
            act.wait_ge(s["ge_ready"], 1)
            act.activation(gt[:, :, :], lg[:, :, :], ACT.Exp).then_inc(s["gx_ready"], 1)
            act.wait_ge(s["ge_ready"], 2)
            act.activation(tw[:, :, 1], tw[:, :, 0], ACT.Exp, scale=0.5).then_inc(s["gx_ready"], 1)

            def silu(k, c, bias):
                for f in range(NF):
                    act.wait_ge(s["up_ready"], NF * k + f + 1)
                    if f == 0 and (not isinstance(k, int) or k >= 2):
                        act.wait_ge(s["dn_ready"], k - 1)
                    act.activation(sT[:, c % 2, f, 0:512], sc[:, f, :], ACT.Silu,
                                   bias=bias[:, f:f + 1]).then_inc(s["silu_done"], 1)

            act.wait_ge(s["w2_in"], 16 * 9)
            for c in range(STEPS):
                silu(c, c, b1_sb[:, NF * NE:NF * NE + NF])
            with act.Fori(0, NE // 2) as u:
                for p in range(2):
                    e = 2 * u + p
                    act.wait_ge(s["cur_ready"], e + 1)
                    for c in range(STEPS):
                        silu(STEPS * (e + 1) + c, c, bcur[:, p, :])

        @block.vector
        def _(dve):
            link = [0]

            def chained(ins):
                link[0] += 1
                ins.then_inc(s["chain_v"], 1)
                dve.wait_ge(s["chain_v"], link[0])

            def tile_stats(n):
                dve.bn_stats(stats[:, n, :], x_sb[:, n, :])

            def rstd(ns, wait):
                dve.wait_ge(*wait)
                chained(dve.reciprocal(rst[:, ns], std[:, ns]))
                chained(dve.tensor_tensor(nwt[:, ns], rst[:, ns], rst[:, ns], ALU.mult))
                chained(dve.tensor_tensor(nwt[:, ns], nwt[:, ns], var[:, ns], ALU.mult))
                chained(dve.tensor_scalar(nwt[:, ns], nwt[:, ns], -0.5, 1.5, ALU.mult, ALU.add))
                chained(dve.tensor_tensor(rst[:, ns], rst[:, ns], nwt[:, ns], ALU.mult))

            def aggregate(ns, done):
                ins = None
                for n in ns:
                    ins = dve.bn_stats(stats[:, n, :], x_sb[:, n, :])
                chained(ins)
                for n in ns:
                    ins = dve.bn_aggr(mv[:, n, :], stats[:, n, :])
                chained(ins)
                dve.tensor_scalar(var[:, ns[0]:ns[-1] + 1], mv[:, ns[0]:ns[-1] + 1, 1], EPS, None,
                                  ALU.add).then_inc(done, 1)

            def normalise(n, done):
                dve.tensor_scalar(xn[:, n, :], x_sb[:, n, :], mv[:, n, 0:1], rst[:, n:n + 1], ALU.subtract,
                                  ALU.mult).then_inc(done, 1)

            dve.wait_ge(x_in[0], 16)
            aggregate(list(range(8)), s["var_ready"])
            dve.wait_ge(s["cs_ready"], 1)
            for b in range(B):
                ins = dve.tensor_copy(csB[:, b, :], cs[:, b:b + 1].broadcast_to([P, P]))
            ins.then_inc(s["csb_ready"], 1)
            dve.wait_ge(s["comp_ready"], 1)
            dve.tensor_copy(wqkv[:, :, :], aux[:, 0, 0:384].rearrange("p (a c) -> p a c", a=3)).then_inc(s["wqkv_ready"], 1)
            rstd(slice(0, 8), (s["std_ready"], 1))
            for n in range(8):
                normalise(n, s["xn_ready"])
            dve.wait_ge(s["mod_ready"], 1)
            chained(dve.tensor_copy(modT[:, :, :], aux[:, 1, 0:12].rearrange("p (j b) -> p j b", b=B)))
            for k in range(2):
                ins = dve.tensor_scalar(scl[:, k, :], modT[:, 3 * k + 1, :], 1.0, None, ALU.add)
            ins.then_inc(s["mod_done"], 1)
            gps = oacc[:, 0, :].rearrange("p (k b c) -> p k b c", k=2, b=B)
            chained(dve.tensor_scalar(gsgn[:, :, :, :], gps, 0.0, 2.0, ALU.is_ge, ALU.mult))
            chained(dve.tensor_scalar(gsgn[:, :, :, :], gsgn[:, :, :, :], -1.0, None, ALU.add))
            chained(dve.tensor_tensor(gabs[:, :, :, :], gps, gsgn[:, :, :, :], ALU.mult))
            chained(dve.scalar_tensor_tensor(out=gB[:, :, :, :], in0=gabs[:, :, :, :], scalar=0.25,
                                             in1=gsgn[:, :, :, :], op0=ALU.max, op1=ALU.mult))
            for b in range(B):
                ins = dve.tensor_tensor(wog[:, b, :], wo_sb[:, :], gB[:, 0, b, :], ALU.mult)
            ins.then_inc(s["wog_ready"], 1)

            def residue(n):
                b, kq, half = QK[n]
                dve.wait_ge(s["hi_ready"], n + 1)
                if n >= 2:
                    dve.wait_ge(s["lo_ready"], n - 1)
                dve.tensor_tensor(r1[:, n % 2, :], qk_bank[n % 3],
                                  parts[:, kq, 0, b * S + 512 * half:b * S + 512 * half + 512],
                                  ALU.subtract).then_inc(s["r1_ready"], 1)

            for n in range(4):
                residue(n)
            dve.wait_ge(x_in[1], 16)
            aggregate(list(range(8, 16)), s["var_ready"])
            rstd(slice(8, 16), (s["std_ready"], 2))
            for n in range(8, 16):
                normalise(n, s["xn_ready"])
            for n in range(4, 8):
                residue(n)

            def partial_maxima(a0, p):
                for k, (h, i, k0, w, diagonal, place) in enumerate(MAXU):
                    bank = aux[:, (a0[1] + k) % 2, 0:w]
                    at = mxp[:, p, 8 * h + i, place:place + 1]
                    dve.wait_ge(s["aux_ready"], a0[0] + k + 1)
                    if diagonal:
                        dve.sem_inc(s["passed_v"], 1)
                        ins = dve.tensor_tensor_reduce(bank, bank, slab[:, 512 - w:512], 1.0, LOWEST,
                                                       ALU.add, ALU.max, at)
                    else:
                        ins = dve.tensor_reduce(at, bank, AX_X, ALU.max)
                    ins.then_inc(s["aux_free"], 1)
                dve.wait_ge(s["aux_free"], a0[0] + NM)

            def maxima(p):
                dve.tensor_reduce(negm[:, :], mxp[:, p, :, :], AX_X, ALU.max, negate=True).then_inc(s["negm_ready"], 1)

            def neg_out(a, par):
                dve.wait_ge(s["aux_ready"], a + 1)
                dve.tensor_copy(negT[:, :], aux[0:96, par, 0:64].bitcast(BF16)).then_inc(s["aux_free"], 1)

            def attn_out(u, p, c, a, par, v):
                dve.wait_ge(s["aux_ready"], a + 1)
                ps = aux[:, par, :].rearrange("p (i h c) -> p i h c", i=4, h=HQ)
                dve.reciprocal(rden[:, c, :, :], ps[:, :, :, DK]).then_inc(s["chain_v"], 1)
                dve.wait_ge(s["chain_v"], v + 1)
                dst = attn[:, 8 * p + 4 * c:8 * p + 4 * c + 4, bass.ds(HQ * DK * u, HQ * DK)]
                dve.tensor_tensor(dst.rearrange("p i (h c) -> p i h c", h=HQ), ps[:, :, :, 0:DK],
                                  rden[:, c, :, :].unsqueeze(3).broadcast_to([P, 4, HQ, DK]),
                                  ALU.mult).then_inc(s["aux_free"], 1)

            dve.wait_ge(s["const_ready"], 5)
            partial_maxima((0, 0), 0)
            maxima(0)
            neg_out(NM, NM % 2)
            base = link[0]

            def body(t, u, p, more):
                a0 = AUX0 + AUXN * t
                par = (AUX0 + AUXN * p) % 2
                if more:
                    partial_maxima((a0, par), 1 - p)
                    dve.wait_ge(s["neg3_ready"], t + 1)
                    maxima(1 - p)
                    dve.wait_ge(s["negrow"], 16 * t + 16)
                    neg_out(a0 + NM, (par + NM) % 2)
                n = NM + 1 if more else 0
                for c in range(2):
                    attn_out(u, p, c, a0 + n + c, (par + n + c) % 2, base + 2 * t + c)

            with dve.Fori(0, T // 2 - 1) as u:
                for p in range(2):
                    body(2 * u + p, u, p, True)
            body(T - 2, T // 2 - 1, 0, True)
            body(T - 1, T // 2 - 1, 1, False)
            link[0] = base + 2 * T

            for g in range(4):
                dve.wait_ge(s["pj_ready"], g + 1)
                ins = dve.tensor_tensor(x_sb[:, 4 * g:4 * g + 4, :], oacc[:, g % 2, :].rearrange("p (n c) -> p n c", n=4),
                                        x_sb[:, 4 * g:4 * g + 4, :], ALU.add)
                ins.then_inc(s["x2_done"], 1)
            dve.wait_ge(s["x2_done"], 4)
            aggregate(list(range(NT)), s["var2_ready"])
            rstd(slice(0, NT), (s["std2_ready"], 1))
            for n in range(NT):
                normalise(n, s["xn2_ready"])
            dve.wait_ge(s["lg_ready"], 4)
            chained(dve.tensor_copy(lg[:, :, :], oacc[:, 1, 0:NT * NE].rearrange("p (n e) -> p n e", e=NE)))
            chained(dve.tensor_reduce(gmx[:, :], lg[:, :, :], AX_X, ALU.max))
            dve.tensor_tensor(lg[:, :, :], lg[:, :, :], gmx[:, :].unsqueeze(2).broadcast_to([P, NT, NE]),
                              ALU.subtract).then_inc(s["ge_ready"], 1)
            dve.wait_ge(s["gx_ready"], 1)
            chained(dve.tensor_reduce(gsm[:, :], gt[:, :, :], AX_X, ALU.add))
            chained(dve.reciprocal(gsm[:, :], gsm[:, :]))
            chained(dve.tensor_tensor(gt[:, :, :], gt[:, :, :], gsm[:, :].unsqueeze(2).broadcast_to([P, NT, NE]),
                                      ALU.mult))
            for n in range(NT):
                ins = dve.max(top[:, n, :], gt[:, n, :])
            chained(ins)
            for n in range(NT):
                ins = dve.max_index(topi[:, n, :], top[:, n, :], gt[:, n, :])
            chained(ins)
            dve.tensor_copy(topf[:, :, :], topi[:, :, 0:2])
            dve.tensor_tensor(tw[:, :, 0], top[:, :, 1], top[:, :, 0], ALU.subtract).then_inc(s["ge_ready"], 1)
            dve.wait_ge(s["gx_ready"], 2)
            chained(dve.tensor_scalar(tw[:, :, 0], tw[:, :, 1], 1.0, None, ALU.add))
            chained(dve.reciprocal(tw[:, :, 0], tw[:, :, 0]))
            chained(dve.tensor_tensor(tw[:, :, 1], tw[:, :, 1], tw[:, :, 0], ALU.mult))
            io = iota8[:, :].unsqueeze(1).broadcast_to([P, NT, NE])
            for k in range(2):
                dst = wsel[:, :, :] if k else wgt[:, :, 0:NE]
                chained(dve.tensor_tensor(dst, io, topf[:, :, k:k + 1].broadcast_to([P, NT, NE]), ALU.is_equal))
                chained(dve.tensor_tensor(dst, dst, tw[:, :, k:k + 1].broadcast_to([P, NT, NE]), ALU.mult))
            dve.tensor_tensor(wgt[:, :, 0:NE], wgt[:, :, 0:NE], wsel[:, :, :], ALU.add).then_inc(s["wgt_ready"], 1)
            for g in range(4):
                dve.wait_ge(s["wt_ready"], g + 1)
                dve.tensor_copy(wT[:, 512 * g:512 * g + 512], aux[0:NE + 1, g % 2, :]).then_inc(s["wT_ready"], 1)

            def down_bank(c):
                return oacc[:, c % 2, :].rearrange("p (n c) -> p n c", n=4)

            for c in range(STEPS):
                dve.wait_ge(s["dn_ready"], c + 1)
                dve.tensor_copy(acc[:, 4 * c:4 * c + 4, :], down_bank(c)).then_inc(s["acc_done"], 1)

            def expert(k0, p, last):
                for c in range(STEPS):
                    dve.wait_ge(s["acc_done"], k0 + c - 3)
                    dve.wait_ge(s["dn_ready"], k0 + c + 1)
                    for i in range(4):
                        n = 4 * c + i
                        ins = dve.scalar_tensor_tensor(out=acc[:, n, :], in0=down_bank(c)[:, i, :],
                                                       scalar=wcur[:, p, n:n + 1], in1=acc[:, n, :],
                                                       op0=ALU.mult, op1=ALU.add)
                    ins.then_inc(s["acc_done"], 1)
                    if last:
                        dve.wait_ge(s["acc_done"], k0 + c + 1)
                        tiles = slice(4 * c, 4 * c + 4)
                        gate = gB[:, 1, c // 2:c // 2 + 1, :].broadcast_to([P, 4, C])
                        chained(dve.tensor_tensor(acc[:, tiles, :], acc[:, tiles, :], gate, ALU.mult))
                        dve.tensor_tensor(yout[:, tiles, :], acc[:, tiles, :], x_sb[:, tiles, :],
                                          ALU.add).then_inc(s["y_ready"], 1)

            with dve.Fori(0, NE // 2 - 1) as u:
                for p in range(2):
                    e = 2 * u + p
                    dve.wait_ge(s["cur_ready"], e + 1)
                    expert(STEPS * (e + 1), p, False)
            for p in range(2):
                e = NE - 2 + p
                dve.wait_ge(s["cur_ready"], e + 1)
                expert(STEPS * (e + 1), p, p == 1)

        @block.tensor
        def _(pe):
            pe.sem_inc(s["pv_done"], 1)
            pe.wait_ge(s["w_in"], 128)
            for k in range(3):
                ins = pe.matmul(aux[:, 0, P * k:P * k + P], wd_sb[:, min(k, 1), :], wu_sb[:, k, :],
                                start=True, stop=True)
            ins.then_inc(s["comp_ready"], 1)
            pe.wait_ge(s["cs_ready"], 1)
            for j in range(6):
                pe.matmul(aux[:, 1, 2 * j:2 * j + 2], wmod_sb[:, C * j:C * j + C], cs[:, :], start=True, stop=True)
            pe.wait_ge(s["csb_ready"], 1)
            for k in range(2):
                for b in range(B):
                    ins = pe.matmul(oacc[:, 0, P * (2 * k + b):P * (2 * k + b) + P], csB[:, b, :],
                                    wmod_sb[:, C * (3 * k + 2):C * (3 * k + 3)], start=True, stop=True)
            ins.then_inc(s["mod_ready"], 1)
            pe.wait_ge(s["const_ready"], 2)

            def x_turn(g):
                if g >= 2:
                    pe.wait_ge(s["hT_ready"], g - 1)
                for i in range(4):
                    n = 4 * g + i
                    pe.wait_ge(s["xn_ready"], n + 1)
                    ins = pe.transpose(sc[:, g % 2, P * i:P * i + P], xn[:, n, :], ident[:, :])
                ins.then_inc(s["xT_ready"], 1)

            def project(n):
                b, kq, half = QK[n]
                pe.wait_ge(s["hT_ready"], 2 * b + half + 1)
                if n >= 3:
                    pe.wait_ge(s["r1_ready"], n - 2)
                pe.matmul(qk_bank[n % 3], wqkv[:, 1 - kq, :], hT[:, b * S + 512 * half:b * S + 512 * half + 512],
                          start=True, stop=True).then_inc(s["qk_ready"], 1)

            def project_v(g):
                if g >= 2:
                    pe.wait_ge(s["v_done"], g - 1)
                elif g == 1:
                    pe.wait_ge(s["mod_done"], 1)
                for i in range(4):
                    n = 4 * g + i
                    ins = pe.matmul(aux[:, g % 2, P * i:P * i + P], hT[:, P * n:P * n + P], wqkv[:, 2, :],
                                    start=True, stop=True)
                ins.then_inc(s["v_ready"], 1)

            x_turn(0)
            x_turn(1)
            pe.wait_ge(s["wqkv_ready"], 1)
            for n in range(4):
                project(n)
            project_v(0)
            project_v(1)
            x_turn(2)
            x_turn(3)
            for n in range(4, 8):
                project(n)
            project_v(2)
            project_v(3)

            def max_scores(a0, par, p, units):
                for k in units:
                    h, i, k0, w, diagonal, place = MAXU[k]
                    a = a0 + k
                    if not isinstance(a, int) or a >= 2:
                        pe.wait_ge(s["aux_free"], a - 1)
                    ins = pe.matmul(aux[:, (par + k) % 2, 0:w], S1[0:CROSS, p, 1, S * h + P * i:S * h + P * i + P],
                                    S1[0:CROSS, p, 0, S * h + k0:S * h + k0 + w], start=True, stop=True)
                    ins.then_inc(s["aux_ready"], 1)

            def turn_max(a, par, n):
                pe.wait_ge(s["neg3_ready"], n)
                pe.wait_ge(s["aux_free"], a - 1)
                pe.transpose(aux[0:96, par, 0:64].bitcast(BF16), neg3[:, :, :].rearrange("p a c -> p (a c)"),
                             identb[:, :]).then_inc(s["aux_ready"], 1)

            def scores(t, slot, p):
                for n, (j, h0, nh, w, pitch) in enumerate(UNITS[slot]):
                    g = NU * t + UBASE[slot] + n
                    if not isinstance(g, int) or g >= 2:
                        pe.wait_ge(s["exp_done"], g - 1)
                    if slot == 0 and n == 0:
                        pe.wait_ge(s["negrow"], 16 * t + 16)
                    buf = (UBASE[slot] + n) % 2
                    dst = sc[:, 2 * buf:2 * buf + 2, :].rearrange("p a c -> p (a c)")
                    for k in range(nh):
                        h = h0 + k
                        for c in range(0, w, 512):
                            m = min(512, w - c)
                            q = S * h + P * j + c
                            pe.matmul(dst[:, pitch * k + c:pitch * k + c + m],
                                            S2[0:NEG_ROW + 3, p, 0, S * h + P * j:S * h + P * j + P],
                                            S2[0:NEG_ROW + 3, p, 1, q:q + m], start=True, stop=True)
                        ins = pe.matmul(dst[:, pitch * k:pitch * k + P], identb[:, :], after[:, :],
                                        start=False, stop=True, skip_group_check=True)
                    ins.then_inc(s["score_ready"], 1)

            def weigh(t, slot, p):
                j = SLOTS[slot]
                pe.wait_ge(s["exp_done"], NU * t + UBASE[slot + 1])
                if slot == 0:
                    pe.wait_ge(s["vb_ready"], t + 1)
                    pe.wait_ge(s["o_done"], 2 * t + 1)
                for c in range(2):
                    q0 = max(512 * c, P * j)
                    if q0 >= 512 * c + 512:
                        continue
                    for h in range(HQ):
                        ins = pe.matmul(oacc[VW * h:VW * h + VW, c, q0 - 512 * c:512], vb[:, p, j, h, :],
                                        pr[:, slot % 2, h, q0:512 * c + 512],
                                        start=(slot == 0), stop=(slot == (6 if c == 0 else 7)))
                ins.then_inc(s["pv_done"], 1)

            def turn_out(t, c, a, par):
                pe.wait_ge(s["o_done"], 2 * t + c + 2)
                pe.wait_ge(s["aux_free"], a - 1)
                for i in range(4):
                    ins = pe.transpose(aux[:, par, P * i:P * i + P], osb[:, c, P * i:P * i + P], ident[:, :])
                ins.then_inc(s["aux_ready"], 1)

            def body(t, u, p, more):
                a0 = AUX0 + AUXN * t
                par = (AUX0 + AUXN * p) % 2
                per = NM // 6
                for slot in range(1, 8):
                    scores(t, slot, p)
                    if slot == 7:
                        pass
                    if more and slot == 1:
                        pe.wait_ge(s1_in[1 - p], 16 * NLOAD * (u + p + 1))
                    if more and slot < 7:
                        max_scores(a0, par, 1 - p, range(per * (slot - 1), per * slot))
                    weigh(t, slot - 1, p)
                if more:
                    turn_max(a0 + NM, (par + NM) % 2, t + 2)
                weigh(t, 7, p)
                n = NM + 1 if more else 0
                for c in range(2):
                    turn_out(t, c, a0 + n + c, (par + n + c) % 2)

            def next_scores(t, u, p):
                pe.wait_ge(s2_in[1 - p], 32 * (u + p + 1))
                scores(t + 1, 0, 1 - p)

            pe.wait_ge(s["v_done"], 4)
            pe.wait_ge(s1_in[0], 16 * NLOAD)
            max_scores(0, 0, 0, range(NM))
            turn_max(NM, NM % 2, 1)
            pe.wait_ge(s2_in[0], 32)
            pe.wait_ge(s["r1_ready"], 8)
            scores(0, 0, 0)
            with pe.Fori(0, T // 2 - 1) as u:
                for p in range(2):
                    body(2 * u + p, u, p, True)
                    next_scores(2 * u + p, u, p)
            body(T - 2, T // 2 - 1, 0, True)
            next_scores(T - 2, T // 2 - 1, 0)
            body(T - 1, T // 2 - 1, 1, False)

            pe.wait_ge(s["exp_done"], NU * T)
            pe.wait_ge(s["aux_free"], AUX0 + AUXN * (T - 1) + 2)
            pe.wait_ge(s["wog_ready"], 1)
            for g in range(5):
                if g < 4:
                    for i in range(4):
                        n = 4 * g + i
                        ins = pe.transpose(sc[:, g, P * i:P * i + P], attn[:, n, :],
                                           ident[:, :])
                    ins.then_inc(s["at_ready"], 1)
                if g:
                    k = g - 1
                    pe.wait_ge(s["at_done"], k + 1)
                    if k >= 2:
                        pe.wait_ge(s["x2_done"], k - 1)
                    else:
                        pe.wait_ge(s["o_done"], 2 * T + 1)
                    for i in range(4):
                        ins = pe.matmul(oacc[:, k % 2, P * i:P * i + P], aT[:, k % 2, P * i:P * i + P], wog[:, k // 2, :],
                                        start=True, stop=True)
                    ins.then_inc(s["pj_ready"], 1)
            pe.wait_ge(s["w2_in"], 16 * 9)
            for g in range(4):
                for i in range(4):
                    n = 4 * g + i
                    pe.wait_ge(s["xn2_ready"], n + 1)
                    ins = pe.transpose(sc[:, g, P * i:P * i + P], xn[:, n, :], ident[:, :])
                ins.then_inc(s["x2T_ready"], 1)
            for g in range(4):
                pe.wait_ge(s["h2T_ready"], g + 1)
                if g >= 2:
                    pe.wait_ge(s["r1T_ready"], g - 1)
                pe.matmul(aux[0:32, g % 2, :], wr1_sb[:, :], h2T[:, 512 * g:512 * g + 512],
                          start=True, stop=True).then_inc(s["rt_ready"], 1)
            for g in range(4):
                pe.wait_ge(s["r1T_ready"], g + 1)
                for i in range(4):
                    n = 4 * g + i
                    ins = pe.matmul(oacc[:, 1, NE * n:NE * n + NE], r1T[:, P * n:P * n + P], wr2_sb[:, :],
                                    start=True, stop=True)
                ins.then_inc(s["lg_ready"], 1)

            def up(k, c, w):
                for f in range(NF):
                    if not isinstance(k, int) or k >= 1:
                        pe.wait_ge(s["silu_done"], NF * k + f - NF + 1)
                    pe.matmul(sc[:, f, :], w[:, P * f:P * f + P], h2T[:, 512 * c:512 * c + 512],
                              start=True, stop=True).then_inc(s["up_ready"], 1)

            def down(k, c, w, shared):
                pe.wait_ge(s["silu_done"], NF * k + NF)
                if not isinstance(k, int) or k >= 2:
                    pe.wait_ge(s["acc_done"], k - 1)
                for i in range(4):
                    n = 4 * c + i
                    dst = oacc[:, c % 2, P * i:P * i + P]
                    if shared:
                        pe.matmul(dst, wT[:, P * n:P * n + P], be2_sb[:, :], start=True, stop=False)
                    for f in range(NF):
                        ins = pe.matmul(dst, sT[:, c % 2, f, P * i:P * i + P], w[:, f, :],
                                        start=(f == 0 and not shared), stop=(f == NF - 1))
                ins.then_inc(s["dn_ready"], 1)

            up(0, 0, sh_up[:, :])
            pe.wait_ge(s["wgt_ready"], 1)
            for g in range(4):
                if g >= 2:
                    pe.wait_ge(s["wT_ready"], g - 1)
                for i in range(4):
                    n = 4 * g + i
                    ins = pe.transpose(aux[0:NE + 1, g % 2, P * i:P * i + P], wgt[:, n, :], ident[:, :])
                ins.then_inc(s["wt_ready"], 1)
            for c in range(1, STEPS):
                up(c, c, sh_up[:, :])
                pe.wait_ge(s["wT_ready"], c)
                down(c - 1, c - 1, sh_dn[:, :, :], True)

            def first_up(k, p):
                up(k, 0, wup[:, p, :])

            pe.wait_ge(ew[0], 32)
            first_up(STEPS, 0)
            pe.wait_ge(s["wT_ready"], 4)
            down(3, 3, sh_dn[:, :, :], True)

            def rest(k0, p):
                for c in range(1, STEPS):
                    up(k0 + c, c, wup[:, p, :])
                    down(k0 + c - 1, c - 1, wdn[:, p, :, :], False)

            def finish(k0, p, count):
                pe.wait_ge(ew[1 - p], count)
                first_up(k0 + STEPS, 1 - p)
                down(k0 + 3, 3, wdn[:, p, :, :], False)

            with pe.Fori(0, NE // 2 - 1) as u:
                for p in range(2):
                    k0 = STEPS * (2 * u + p + 1)
                    rest(k0, p)
                    finish(k0, p, 32 * (u + p + 1))
            k0 = STEPS * (NE - 1)
            rest(k0, 0)
            finish(k0, 0, 32 * (NE // 2))
            rest(k0 + STEPS, 1)
            down(k0 + STEPS + 3, 3, wdn[:, 1, :, :], False)


def kernel(**inputs):
    import numpy as _np
    import concourse.bacc as _bacc
    from concourse import mybir as _mybir
    from concourse.bass_utils import run_bass_kernel_spmd as _run

    a = {k.replace("L0_", ""): _np.asarray(v) for k, v in inputs.items()}
    row = lambda v: v.reshape(1, -1)
    NE, F = a["ffn_be1"].shape
    biases = _np.concatenate([a["ffn_be1"], row(a["ffn_bs1"])], 0).reshape(NE + 1, F // 128, 128)
    data = {
        "x": a["attn_x"], "cT": a["c"].T, "wmod": a["wmod"], "wdqT": a["attn_W_dq"].T, "wdkvT": a["attn_W_dkv"].T,
        "wuq": a["attn_W_uq"], "wuk": a["attn_W_uk"], "wuv": a["attn_W_uv"], "wo": a["attn_W_o"],
        "wr1": a["ffn_Wr1"], "br1": a["ffn_br1"].reshape(-1, 1), "wr2": a["ffn_Wr2"], "br2": row(a["ffn_br2"]),
        "ws1": a["ffn_Ws1"], "ws2": a["ffn_Ws2"], "bs2": row(a["ffn_bs2"]), "we1": a["ffn_We1"], "we2": a["ffn_We2"],
        "be2": a["ffn_be2"], "b1T": biases.transpose(2, 0, 1).reshape(128, -1),
    }
    nc = _bacc.Bacc("TRN2", target_bir_lowering=False, num_devices=1)
    arrays, args = {}, []
    for name, v in data.items():
        v = _np.ascontiguousarray(v)
        arrays[f"in_{name}"] = v
        args.append(nc.dram_tensor(f"in_{name}", v.shape, _mybir.dt.from_np(v.dtype), kind="ExternalInput").ap())
    out = nc.dram_tensor("out_y", a["attn_x"].shape, _mybir.dt.float32, kind="ExternalOutput").ap()
    adaln_layer(nc, *args, out)
    r = _run(nc, [arrays], core_ids=[0])
    return r.results[0]["out_y"]
```

```python
from contextlib import ExitStack

import concourse.bass as bass
from concourse import mybir

ALU = mybir.AluOpType
ACT = mybir.ActivationFunctionType
AX_X = mybir.AxisListType.X
F32 = mybir.dt.float32
BF16 = mybir.dt.bfloat16
U32 = mybir.dt.uint32

P = 128
LOWEST = -3.0e38
EPS = 1e-5

SLOTS = [0, 7, 1, 6, 2, 5, 3, 4]
HQ = 4
DK = 8
VW = 32
NEG_ROW = 96
CROSS = 72


def score_units():
    out = []
    for j in SLOTS:
        w = 1024 - P * j
        n = 1 if w > 512 else (2 if w > 256 else 4)
        pitch = 1024 // n if w > 256 or n == 1 else w
        out.append([(j, h, n, w, pitch) for h in range(0, HQ, n)])
    return out


def max_units():
    out = []
    for i in range(8):
        w = P * (i + 1)
        if w > 512:
            out += [(i, 0, 512, False, 0), (i, 512, w - 512, True, 1)]
        else:
            out.append((i, 0, w, True, 0))
    return out


def pair_steps(q):
    units = score_units()
    return [(slot, n) for slot in (2 * q, 2 * q + 1) for n in range(len(units[slot]))]


TURN = (1, 2, 3, 0)


def aux_plan(nm, more, ahead):
    plan = {}
    for q in TURN:
        steps = len(pair_steps(q))
        units = []
        if q in (1, 2) and more:
            units = [("max", 1, nm // 2 + (q - 1) * nm // 4 + k) for k in range(nm // 4)]
        if q in (3, 0) and ahead:
            units = [("max", 2, (0 if q == 3 else nm // 4) + k) for k in range(nm // 4)]
        n = len(units)
        plan[q] = [units[n * i // steps:n * (i + 1) // steps] for i in range(steps)]
    if more:
        plan[3][TURN_STEP].append(("turn", 0, 0))
        plan[0][3].append(("out", 0, 0))
        plan[0][4].append(("out", 1, 0))
    return plan


TURN_STEP = 3


def adaln_layer(nc, x, cT, wmod, wdqT, wdkvT, wuq, wuk, wuv, wo, wr1, br1, wr2, br2,
                ws1, ws2, bs2, we1, we2, be2, b1T, out):
    B, S, C = x.shape
    assert (B, S, C) == (2, 1024, 128)
    NT = B * S // P
    NE = we1.shape[0]
    FF = ws1.shape[1]
    NF = FF // P
    NQ = 16 // HQ
    T = B * NQ
    UNITS = score_units()
    NU = sum(len(u) for u in UNITS)
    UBASE = [sum(len(u) for u in UNITS[:s]) for s in range(9)]
    MAXU = [(h, *m) for h in range(HQ) for m in max_units()]
    NM = len(MAXU)
    AUX0 = NM + NM // 2 + 1
    AUXN = NM + 3
    FULL = aux_plan(NM, True, True)
    NOT_AHEAD = aux_plan(NM, True, False)
    TURNED = NM // 2 + sum(len(x) for x in FULL[3][:TURN_STEP]) + len(FULL[3][TURN_STEP]) - 1
    FIRST = 4
    NLOAD = 12
    STEPS = 4

    with ExitStack() as ctx:
        def sb(name, shape, dt):
            return ctx.enter_context(nc.sbuf_tensor(name, shape, dt))

        def sem(name):
            return ctx.enter_context(nc.semaphore(name))

        sc = ctx.enter_context(nc.psum_tensor("sc", [P, 4, 512], F32))
        aux = ctx.enter_context(nc.psum_tensor("aux", [P, 2, 512], F32))
        oacc = ctx.enter_context(nc.psum_tensor("oacc", [P, 2, 512], F32))

        x_sb = sb("x_sb", [P, NT, C], F32)
        cT_sb = sb("cT_sb", [P, B], F32)
        cs = sb("cs", [P, B], F32)
        csB = sb("csB", [P, B, P], F32)
        wmod_sb = sb("wmod_sb", [P, 6 * C], F32)
        wd_sb = sb("wd_sb", [32, 2, C], F32)
        wu_sb = sb("wu_sb", [32, 3, C], F32)
        wo_sb = sb("wo_sb", [P, C], F32)
        wr1_sb = sb("wr1_sb", [P, 32], F32)
        br1_sb = sb("br1_sb", [32, 1], F32)
        wr2_sb = sb("wr2_sb", [33, NE], F32)
        be2_sb = sb("be2_sb", [NE + 1, C], F32)
        b1_sb = sb("b1_sb", [P, (NE + 1) * NF], F32)
        ident = sb("ident", [P, P], F32)
        identb = sb("identb", [P, P], BF16)
        after = sb("after", [P, P], BF16)
        slab = sb("slab", [P, 512], F32)
        iota8 = sb("iota8", [P, NE], F32)
        wqkv = sb("wqkv", [P, 3, C], F32)
        modT = sb("modT", [P, 6, B], F32)
        scl = sb("scl", [P, 2, B], F32)
        gB = sb("gB", [P, 2, B, C], F32)
        wog = sb("wog", [P, B, C], F32)
        stats = sb("stats", [P, NT, 6], F32)
        mv = sb("mv", [P, NT, 2], F32)
        var = sb("var", [P, NT], F32)
        std = sb("std", [P, NT], F32)
        rst = sb("rst", [P, NT], F32)
        nwt = sb("nwt", [P, NT], F32)
        hT = sb("hT", [P, NT * P], F32)
        parts = sb("parts", [P, 2, 3, NT * P], BF16)
        valt = sb("valt", [P, NT, C], F32)
        S1 = sb("S1", [P, 2, 2, HQ * S], BF16)
        S2 = sb("S2", [P, 2, 2, HQ * S], BF16)
        vb = sb("vb", [P, 2, 8, HQ, VW], F32)
        pr = sb("pr", [P, 2, HQ, S], F32)
        prs = sb("prs", [P, HQ, 512], F32)
        mxp = sb("mxp", [P, 2, HQ * 8, 2], F32)
        negm = sb("negm", [P, HQ * 8], F32)
        negr = sb("negr", [P, HQ * 8], F32)
        gsgn, gabs = (pr[:, 0, k, 0:2 * B * C].rearrange("p (k b c) -> p k b c", k=2, b=B) for k in range(2))
        neg3 = sb("neg3", [P, 3, HQ * 8], BF16)
        negT = sb("negT", [96, P], BF16)
        osb = sb("osb", [P, 2, 512], F32)
        r1 = osb
        rden = sb("rden", [P, 2, 4, HQ], F32)
        attn = sb("attn", [P, NT, C], F32)
        xn = attn
        aT = S1[:, 0, :, :].rearrange("p a n -> p (a n)").bitcast(F32)[:, 0:1024].rearrange("p (a n) -> p a n", a=2)
        sT = pr
        wup = S2[:, 0, 0, :].bitcast(F32)[:, 0:2 * FF].rearrange("p (a n) -> p a n", a=2)
        wdn = S2[:, 0, 1, :].bitcast(F32)[:, 0:2 * FF].rearrange("p (a f c) -> p a f c", a=2, f=NF)
        acc = S2[:, 1, 0, :].bitcast(F32).rearrange("p (n c) -> p n c", c=C)
        yout = S2[:, 1, 1, :].bitcast(F32).rearrange("p (n c) -> p n c", c=C)
        h2T = hT
        r1T = sb("r1T", [33, NT * P], F32)
        lg = sb("lg", [P, NT, NE], F32)
        gt = sb("gt", [P, NT, NE], F32)
        gmx = sb("gmx", [P, NT], F32)
        gsm = sb("gsm", [P, NT], F32)
        top = sb("top", [P, NT, 8], F32)
        topi = sb("topi", [P, NT, 8], U32)
        topf = sb("topf", [P, NT, 2], F32)
        tw = sb("tw", [P, NT, 2], F32)
        wgt = sb("wgt", [P, NT, NE + 1], F32)
        wsel = sb("wsel", [P, NT, NE], F32)
        wT = S1[0:NE + 1, 1, 0, :].bitcast(F32)
        wcur = sb("wcur", [P, 2, NT], F32)
        bcur = sb("bcur", [P, 2, NF], F32)
        sh_up = sb("sh_up", [P, FF], F32)
        sh_dn = sb("sh_dn", [P, NF, C], F32)

        kd = nc.dram_tensor("k_parts", [T, HQ, 3, DK, S], BF16, kind="Internal").ap()
        qd = nc.dram_tensor("q_parts", [T, HQ, 3, DK, S], BF16, kind="Internal").ap()

        names = """x_in0 x_in1 w_in w2_in parts_out0 parts_out1 s1_in0 s1_in1 s2_in0 s2_in1 negrow y_out ew0 ew1
            const_ready pad_ready chain_v chain_p chain_a cs_ready csb_ready comp_ready wqkv_ready mod_ready mod_done
            var_ready std_ready xn_ready xT_ready hT_ready qk_ready hi_ready r1_ready mid_ready lo_ready
            v_ready v_done aux_ready aux_free negm_ready neg3_ready score_ready exp_done
            vb_ready pv_done o_done out_turned at_ready at_done pj_ready x2_done var2_ready std2_ready
            xn2_ready x2T_ready h2T_ready rt_ready r1T_ready lg_ready ge_ready gx_ready gp_ready wgt_ready wt_ready
            wT_ready up_ready silu_done dn_ready acc_done cur_ready y_ready wog_ready
            passed_v passed_s passed_p""".split()
        s = {n: sem(n) for n in names}
        x_in = [s["x_in0"], s["x_in1"]]
        parts_out = [s["parts_out0"], s["parts_out1"]]
        s1_in = [s["s1_in0"], s["s1_in1"]]
        s2_in = [s["s2_in0"], s["s2_in1"]]
        ew = [s["ew0"], s["ew1"]]

        block = ctx.enter_context(nc.Block())

        QK = [(b, kq, half) for b in range(B) for kq in range(2) for half in range(2)]
        qk_bank = [sc[:, 2, :], sc[:, 3, :], oacc[:, 1, :]]

        @block.sync
        def _(sp):
            xv = x.rearrange("b (n p) c -> b p n c", p=P)
            sp.dma_start(x_sb[:, 0:8, :], xv[0]).then_inc(x_in[0], 16)
            sp.dma_start(x_sb[:, 8:16, :], xv[1]).then_inc(x_in[1], 16)
            for dst, src in ((wr1_sb[:, :], wr1), (br1_sb[:, :], br1), (wr2_sb[0:32, :], wr2),
                             (wr2_sb[32:33, :], br2), (be2_sb[0:NE, :], be2), (be2_sb[NE:NE + 1, :], bs2),
                             (b1_sb[:, :], b1T), (sh_up[:, :], ws1),
                             (sh_dn[:, :, :], ws2.rearrange("(f p) c -> p f c", p=P))):
                sp.dma_start(dst, src).then_inc(s["w2_in"], 16)

            def store_parts(b):
                for kq, dst in ((0, kd), (1, qd)):
                    for part in range(3):
                        done = 4 * b + 2 * kq + 2
                        sp.wait_ge((s["hi_ready"], s["mid_ready"], s["lo_ready"])[part], done)
                        sp.dma_start(
                            dst[NQ * b:NQ * b + NQ, :, part, :, :].rearrange("t h d n -> (t h) d n"),
                            parts[:, kq, part, b * S:(b + 1) * S]).then_inc(parts_out[b], 16)

            def load_s1(u, p):
                sp.wait_ge(parts_out[p], 96)
                sp.sem_inc(s["passed_s"], 1)
                kt = kd[bass.ds(NQ * p + u, 1)].rearrange("t h a d n -> (t h) a d n")
                qt = qd[bass.ds(NQ * p + u, 1)].rearrange("t h a d n -> (t h) a d n")
                for a in range(3):
                    sp.dma_start(S1[24 * a:24 * a + 24, p, 0, :].rearrange("r (h n) -> r h n", h=HQ),
                                 kt.rearrange("h b d n -> (b d) h n")).then_inc(s1_in[p], 16)
                    for b in range(3):
                        r = 24 * a + 8 * b
                        sp.dma_start(S1[r:r + 8, p, 1, :].rearrange("r (h n) -> r h n", h=HQ),
                                     qt[:, a, :, :].rearrange("h d n -> d h n")).then_inc(s1_in[p], 16)

            def copy_s2(p):
                for kq in range(2):
                    sp.dma_start(S2[0:CROSS, p, kq, :], S1[0:CROSS, p, kq, :]).then_inc(s2_in[p], 16)

            def neg_rows(p):
                sp.dma_start(S2[NEG_ROW:NEG_ROW + 3, p, 1, :].rearrange("r (s q) -> r s q", q=P),
                             negT[:, :]).then_inc(s["negrow"], 16)

            store_parts(0)
            load_s1(0, 0)
            sp.wait_ge(s1_in[0], 16 * NLOAD)
            sp.wait_ge(s["pad_ready"], 1)
            copy_s2(0)
            store_parts(1)
            load_s1(0, 1)
            sp.wait_ge(s["aux_free"], NM + FIRST + 1)
            neg_rows(0)
            sp.wait_ge(s2_in[0], 32)
            load_s1(1, 0)

            def body(t, u, p, load, whole=True):
                sp.wait_ge(s1_in[1 - p], 16 * NLOAD * (u + p + 1))
                sp.sem_inc(s["passed_s"], 1)
                sp.wait_ge(s["score_ready"], NU * t + UBASE[2])
                copy_s2(1 - p)
                sp.wait_ge(s["aux_free"], AUX0 + AUXN * t + (TURNED if whole else NM // 2) + 1)
                neg_rows(1 - p)
                if load:
                    sp.wait_ge(s2_in[1 - p], 32 * (u + p + 1))
                    load_s1(u + 1 + p, 1 - p)

            with sp.Fori(0, T // 2 - 2) as u:
                for p in range(2):
                    body(2 * u + p, u, p, True)
            body(T - 4, T // 2 - 2, 0, True)
            body(T - 3, T // 2 - 2, 1, False)
            body(T - 2, T // 2 - 1, 0, False, whole=False)

            sp.wait_ge(s["score_ready"], NU * T)
            with sp.Fori(0, NE // 2) as u:
                for p in range(2):
                    e = 2 * u + p
                    sp.wait_ge(s["dn_ready"], STEPS * e + 1)
                    sp.sem_inc(s["passed_s"], 1)
                    sp.dma_start(wup[:, p:p + 1, :],
                                 we1[bass.ds(e, 1)].rearrange("e c f -> c e f")).then_inc(ew[p], 16)
                    sp.dma_start(wdn[:, p, :, :],
                                 we2[bass.ds(e, 1)].rearrange("e (f p) c -> p (e f) c", p=P)).then_inc(ew[p], 16)
            yv = out.rearrange("b (n p) c -> p (b n) c", p=P)
            for g in range(4):
                sp.wait_ge(s["y_ready"], g + 1)
                sp.dma_start(yv[:, 4 * g:4 * g + 4, :], yout[:, 4 * g:4 * g + 4, :]).then_inc(s["y_out"], 16)
            sp.wait_ge(s["y_out"], 64)

        @block.gpsimd
        def _(pool):
            link = [0]

            def chained(ins):
                link[0] += 1
                ins.then_inc(s["chain_p"], 1)
                pool.wait_ge(s["chain_p"], link[0])

            chained(pool.memset(ident[:, :], 0.0))
            chained(pool.affine_select(out=ident[:, :], in_=ident[:, :], compare_op=ALU.not_equal, fill=1.0,
                                       base=0, pattern=[[-1, P]], channel_multiplier=1))
            pool.tensor_copy(identb[:, :], ident[:, :]).then_inc(s["const_ready"], 1)
            chained(pool.memset(after[:, :], 0.0))
            pool.affine_select(out=after[:, :], in_=after[:, :], compare_op=ALU.is_ge, fill=LOWEST,
                               base=0, pattern=[[1, P]], channel_multiplier=-1).then_inc(s["const_ready"], 1)
            chained(pool.memset(slab[:, :], 0.0))
            pool.affine_select(out=slab[:, 384:512], in_=slab[:, 384:512], compare_op=ALU.is_ge, fill=LOWEST,
                               base=0, pattern=[[-1, P]], channel_multiplier=1).then_inc(s["const_ready"], 1)
            pool.memset(mxp[:, :, :, :], LOWEST).then_inc(s["const_ready"], 1)
            pool.iota(iota8[:, :], pattern=[[1, NE]], base=0, channel_multiplier=0,
                      allow_small_or_imprecise_dtypes=True).then_inc(s["const_ready"], 1)
            pool.wait_ge(s["const_ready"], 5)
            for p in range(2):
                chained(pool.memset(S2[64:128, p, :, :].bitcast(F32), 0.0))
                chained(pool.memset(S2[NEG_ROW:NEG_ROW + 3, p, 0, :], 1.0))
            pool.memset(r1T[32:33, :], 1.0).then_inc(s["pad_ready"], 1)
            pool.wait_ge(s["pad_ready"], 1)
            for n, (b, kq, half) in enumerate(QK):
                cols = slice(b * S + 512 * half, b * S + 512 * half + 512)
                pool.wait_ge(s["mid_ready"], n + 1)
                pool.tensor_tensor(parts[:, kq, 2, cols], r1[:, n % 2, :], parts[:, kq, 1, cols],
                                   ALU.subtract).then_inc(s["lo_ready"], 1)
                if n == 3:
                    chained(pool.memset(vb[:, :, :, :, :], 0.0))
                    chained(pool.memset(vb[:, :, :, :, DK:DK + 1], 1.0))
            chained(pool.memset(wgt[:, :, NE:NE + 1], 1.0))

            def split_max(v):
                pool.sem_inc(s["passed_p"], 1)
                pool.tensor_copy(neg3[:, 0, :], negm[:, :]).then_inc(s["chain_p"], 1)
                pool.wait_ge(s["chain_p"], v + 1)
                pool.tensor_tensor(negr[:, :], negm[:, :], neg3[:, 0, :], ALU.subtract).then_inc(s["chain_p"], 1)
                pool.wait_ge(s["chain_p"], v + 2)
                pool.sem_inc(s["passed_p"], 1)
                pool.tensor_copy(neg3[:, 1, :], negr[:, :]).then_inc(s["chain_p"], 1)
                pool.wait_ge(s["chain_p"], v + 3)
                pool.tensor_tensor(neg3[:, 2, :], negr[:, :], neg3[:, 1, :], ALU.subtract).then_inc(s["neg3_ready"], 1)

            def values(u, p):
                pool.wait_ge(s["v_done"], 4)
                src = valt[:, 8 * p:8 * p + 8, bass.ds(HQ * DK * u, HQ * DK)]
                pool.tensor_copy(vb[:, p, :, :, 0:DK],
                                 src.rearrange("p j (h d) -> p j h d", h=HQ)).then_inc(s["vb_ready"], 1)

            base = link[0]
            values(0, 0)
            pool.wait_ge(s["negm_ready"], 1)
            split_max(base)

            def body(t, u, p):
                pool.wait_ge(s["pv_done"], 8 * t + 1)
                values(u + p, 1 - p)
                pool.wait_ge(s["negm_ready"], t + 2)
                split_max(base + 3 * t + 3)

            with pool.Fori(0, T // 2 - 1) as u:
                for p in range(2):
                    body(2 * u + p, u, p)
            body(T - 2, T // 2 - 1, 0)

            pool.wait_ge(s["wgt_ready"], 1)
            pool.wait_ge(s["w2_in"], 16 * 9)
            with pool.Fori(0, NE // 2) as u:
                for p in range(2):
                    e = 2 * u + p
                    pool.wait_ge(s["acc_done"], STEPS * e + 1)
                    pool.wait_ge(s["silu_done"], NF * STEPS * e + 1)
                    pool.tensor_copy(wcur[:, p, :], wgt[:, :, bass.ds(e, 1)].rearrange("p n e -> p (n e)"))
                    pool.tensor_copy(bcur[:, p, :], b1_sb[:, bass.ds(NF * e, NF)]).then_inc(s["cur_ready"], 1)

        @block.scalar
        def _(act):
            act.sem_inc(s["o_done"], 1)
            for dst, src in ((cT_sb[:, :], cT), (wmod_sb[:, :], wmod), (wd_sb[:, 0, :], wdqT), (wd_sb[:, 1, :], wdkvT),
                             (wu_sb[:, 0, :], wuq), (wu_sb[:, 1, :], wuk), (wu_sb[:, 2, :], wuv), (wo_sb[:, :], wo)):
                act.dma_start(dst, src).then_inc(s["w_in"], 16)
            act.wait_ge(s["w_in"], 128)
            act.activation(cs[:, :], cT_sb[:, :], ACT.Silu).then_inc(s["cs_ready"], 1)

            def root(b):
                act.wait_ge(s["var_ready"], b + 1)
                act.activation(std[:, 8 * b:8 * b + 8], var[:, 8 * b:8 * b + 8], ACT.Sqrt).then_inc(s["std_ready"], 1)

            def h_out(g):
                act.wait_ge(s["xT_ready"], g + 1)
                if g == 0:
                    act.wait_ge(s["mod_done"], 1)
                act.activation(hT[:, 512 * g:512 * g + 512], sc[:, g % 2, :], ACT.Identity,
                               bias=modT[:, 0, g // 2:g // 2 + 1],
                               scale=scl[:, 0, g // 2:g // 2 + 1]).then_inc(s["hT_ready"], 1)

            def hi(n):
                b, kq, half = QK[n]
                act.wait_ge(s["qk_ready"], n + 1)
                act.activation(parts[:, kq, 0, b * S + 512 * half:b * S + 512 * half + 512], qk_bank[n % 3],
                               ACT.Copy).then_inc(s["hi_ready"], 1)

            def mid(n):
                b, kq, half = QK[n]
                act.wait_ge(s["r1_ready"], n + 1)
                act.activation(parts[:, kq, 1, b * S + 512 * half:b * S + 512 * half + 512], r1[:, n % 2, :],
                               ACT.Copy).then_inc(s["mid_ready"], 1)

            def v_out(g):
                act.wait_ge(s["v_ready"], g + 1)
                act.activation(
                    valt[:, 4 * g:4 * g + 4, :], aux[:, g % 2, :].rearrange("p (n c) -> p n c", n=4),
                    ACT.Copy).then_inc(s["v_done"], 1)

            for b in range(B):
                root(b)
                h_out(2 * b)
                h_out(2 * b + 1)
                for k in range(4):
                    hi(4 * b + k)
                    if k:
                        mid(4 * b + k - 1)
                mid(4 * b + 3)
                v_out(2 * b)
                v_out(2 * b + 1)

            def exps(t, q, steps):
                for slot, n in steps:
                    j, h, nh, w, pitch = UNITS[slot][n]
                    g = NU * t + UBASE[slot] + n
                    if n == 0:
                        used = 8 * t + (2 * q + 1 if slot % 2 else 2 * q - 2)
                        if not isinstance(t, int) or used > 1:
                            act.wait_ge(s["pv_done"], used)
                    act.wait_ge(s["score_ready"], g + 1)
                    buf = (UBASE[slot] + n) % 2
                    src = sc[:, 2 * buf:2 * buf + 2, :].rearrange("p a c -> p (a c)")
                    src = src[:, 0:nh * pitch].rearrange("p (h c) -> p h c", h=nh)[:, :, 0:w]
                    if slot % 2:
                        dst = prs[:, h:h + nh, P * j - 512:P * j - 512 + w]
                    else:
                        dst = pr[:, q % 2, h:h + nh, P * j:P * j + w]
                    act.activation(dst, src, ACT.Exp, scale=float(DK) ** -0.5).then_inc(s["exp_done"], 1)

            def o_out(t, c):
                act.wait_ge(s["pv_done"], 8 * t + 8 + c)
                if not isinstance(t, int) or t >= 1:
                    act.wait_ge(s["out_turned"], 2 * t + 1 + c)
                act.activation(osb[:, c, :], oacc[:, c, :], ACT.Copy).then_inc(s["o_done"], 1)

            exps(0, 0, pair_steps(0))

            def body(t, last=False):
                for q in (1, 2, 3):
                    exps(t, q, pair_steps(q))
                if not last:
                    exps(t + 1, 0, pair_steps(0)[0:2])
                o_out(t, 0)
                if not last:
                    exps(t + 1, 0, pair_steps(0)[2:3])
                o_out(t, 1)
                if not last:
                    exps(t + 1, 0, pair_steps(0)[3:])

            with act.Fori(0, T // 2 - 1) as u:
                for p in range(2):
                    body(2 * u + p)
            body(T - 2)
            body(T - 1, last=True)

            for g in range(4):
                act.wait_ge(s["at_ready"], g + 1)
                if g >= 2:
                    act.wait_ge(s["pj_ready"], g - 1)
                act.activation(aT[:, g % 2, :], sc[:, g, :], ACT.Copy).then_inc(s["at_done"], 1)
            act.wait_ge(s["var2_ready"], 1)
            act.activation(std[:, :], var[:, :], ACT.Sqrt).then_inc(s["std2_ready"], 1)
            for g in range(4):
                act.wait_ge(s["x2T_ready"], g + 1)
                act.activation(h2T[:, 512 * g:512 * g + 512], sc[:, g, :], ACT.Identity,
                               bias=modT[:, 3, g // 2:g // 2 + 1],
                               scale=scl[:, 1, g // 2:g // 2 + 1]).then_inc(s["h2T_ready"], 1)
                act.wait_ge(s["rt_ready"], g + 1)
                act.activation(r1T[0:32, 512 * g:512 * g + 512], aux[0:32, g % 2, :], ACT.Relu,
                               bias=br1_sb[:, 0:1]).then_inc(s["r1T_ready"], 1)
            act.wait_ge(s["ge_ready"], 1)
            act.activation(gt[:, :, :], lg[:, :, :], ACT.Exp).then_inc(s["gx_ready"], 1)
            act.wait_ge(s["ge_ready"], 2)
            act.activation(tw[:, :, 1], tw[:, :, 0], ACT.Exp, scale=0.5).then_inc(s["gx_ready"], 1)

            def silu(k, c, bias):
                for f in range(NF):
                    act.wait_ge(s["up_ready"], NF * k + f + 1)
                    if f == 0 and (not isinstance(k, int) or k >= 2):
                        act.wait_ge(s["dn_ready"], k - 1)
                    act.activation(sT[:, c % 2, f, 0:512], sc[:, f, :], ACT.Silu,
                                   bias=bias[:, f:f + 1]).then_inc(s["silu_done"], 1)

            act.wait_ge(s["w2_in"], 16 * 9)
            for c in range(STEPS):
                silu(c, c, b1_sb[:, NF * NE:NF * NE + NF])
            with act.Fori(0, NE // 2) as u:
                for p in range(2):
                    e = 2 * u + p
                    act.wait_ge(s["cur_ready"], e + 1)
                    for c in range(STEPS):
                        silu(STEPS * (e + 1) + c, c, bcur[:, p, :])

        @block.vector
        def _(dve):
            link = [0]

            def chained(ins):
                link[0] += 1
                ins.then_inc(s["chain_v"], 1)
                dve.wait_ge(s["chain_v"], link[0])

            def tile_stats(n):
                dve.bn_stats(stats[:, n, :], x_sb[:, n, :])

            def rstd(ns, wait):
                dve.wait_ge(*wait)
                chained(dve.reciprocal(rst[:, ns], std[:, ns]))
                chained(dve.tensor_tensor(nwt[:, ns], rst[:, ns], rst[:, ns], ALU.mult))
                chained(dve.tensor_tensor(nwt[:, ns], nwt[:, ns], var[:, ns], ALU.mult))
                chained(dve.tensor_scalar(nwt[:, ns], nwt[:, ns], -0.5, 1.5, ALU.mult, ALU.add))
                chained(dve.tensor_tensor(rst[:, ns], rst[:, ns], nwt[:, ns], ALU.mult))

            def aggregate(ns, done):
                ins = None
                for n in ns:
                    ins = dve.bn_stats(stats[:, n, :], x_sb[:, n, :])
                chained(ins)
                for n in ns:
                    ins = dve.bn_aggr(mv[:, n, :], stats[:, n, :])
                chained(ins)
                dve.tensor_scalar(var[:, ns[0]:ns[-1] + 1], mv[:, ns[0]:ns[-1] + 1, 1], EPS, None,
                                  ALU.add).then_inc(done, 1)

            def normalise(n, done):
                dve.tensor_scalar(xn[:, n, :], x_sb[:, n, :], mv[:, n, 0:1], rst[:, n:n + 1], ALU.subtract,
                                  ALU.mult).then_inc(done, 1)

            dve.wait_ge(x_in[0], 16)
            aggregate(list(range(8)), s["var_ready"])
            dve.wait_ge(s["cs_ready"], 1)
            for b in range(B):
                ins = dve.tensor_copy(csB[:, b, :], cs[:, b:b + 1].broadcast_to([P, P]))
            ins.then_inc(s["csb_ready"], 1)
            dve.wait_ge(s["comp_ready"], 1)
            dve.tensor_copy(wqkv[:, :, :], aux[:, 0, 0:384].rearrange("p (a c) -> p a c", a=3)).then_inc(s["wqkv_ready"], 1)
            rstd(slice(0, 8), (s["std_ready"], 1))
            for n in range(8):
                normalise(n, s["xn_ready"])
            dve.wait_ge(s["mod_ready"], 1)
            chained(dve.tensor_copy(modT[:, :, :], aux[:, 1, 0:12].rearrange("p (j b) -> p j b", b=B)))
            for k in range(2):
                ins = dve.tensor_scalar(scl[:, k, :], modT[:, 3 * k + 1, :], 1.0, None, ALU.add)
            ins.then_inc(s["mod_done"], 1)
            gps = oacc[:, 0, :].rearrange("p (k b c) -> p k b c", k=2, b=B)
            chained(dve.tensor_scalar(gsgn[:, :, :, :], gps, 0.0, 2.0, ALU.is_ge, ALU.mult))
            chained(dve.tensor_scalar(gsgn[:, :, :, :], gsgn[:, :, :, :], -1.0, None, ALU.add))
            chained(dve.tensor_tensor(gabs[:, :, :, :], gps, gsgn[:, :, :, :], ALU.mult))
            chained(dve.scalar_tensor_tensor(out=gB[:, :, :, :], in0=gabs[:, :, :, :], scalar=0.25,
                                             in1=gsgn[:, :, :, :], op0=ALU.max, op1=ALU.mult))
            for b in range(B):
                ins = dve.tensor_tensor(wog[:, b, :], wo_sb[:, :], gB[:, 0, b, :], ALU.mult)
            ins.then_inc(s["wog_ready"], 1)

            def residue(n):
                b, kq, half = QK[n]
                dve.wait_ge(s["hi_ready"], n + 1)
                if n >= 2:
                    dve.wait_ge(s["lo_ready"], n - 1)
                dve.tensor_tensor(r1[:, n % 2, :], qk_bank[n % 3],
                                  parts[:, kq, 0, b * S + 512 * half:b * S + 512 * half + 512],
                                  ALU.subtract).then_inc(s["r1_ready"], 1)

            for n in range(4):
                residue(n)
            dve.wait_ge(x_in[1], 16)
            aggregate(list(range(8, 16)), s["var_ready"])
            rstd(slice(8, 16), (s["std_ready"], 2))
            for n in range(8, 16):
                normalise(n, s["xn_ready"])
            for n in range(4, 8):
                residue(n)

            def bank(a):
                return aux[:, a % 2, :]

            def max_unit(k, a, par, p):
                h, i, k0, w, diagonal, place = MAXU[k]
                src = bank(par)[:, 0:w]
                at = mxp[:, p, 8 * h + i, place:place + 1]
                dve.wait_ge(s["aux_ready"], a + 1)
                if diagonal:
                    dve.sem_inc(s["passed_v"], 1)
                    ins = dve.tensor_tensor_reduce(src, src, slab[:, 512 - w:512], 1.0, LOWEST, ALU.add, ALU.max, at)
                else:
                    ins = dve.tensor_reduce(at, src, AX_X, ALU.max)
                ins.then_inc(s["aux_free"], 1)

            def maxima(p, a):
                dve.wait_ge(s["aux_free"], a)
                dve.tensor_reduce(negm[:, :], mxp[:, p, :, :], AX_X, ALU.max, negate=True).then_inc(s["negm_ready"], 1)

            def neg_out(a, par):
                dve.wait_ge(s["aux_ready"], a + 1)
                dve.tensor_copy(negT[:, :], bank(par)[0:96, 0:64].bitcast(BF16)).then_inc(s["aux_free"], 1)

            def attn_out(u, p, c, a, par, v):
                dve.wait_ge(s["aux_ready"], a + 1)
                ps = bank(par).rearrange("p (i h c) -> p i h c", i=4, h=HQ)
                dve.reciprocal(rden[:, c, :, :], ps[:, :, :, DK]).then_inc(s["chain_v"], 1)
                dve.wait_ge(s["chain_v"], v + 1)
                dst = attn[:, 8 * p + 4 * c:8 * p + 4 * c + 4, bass.ds(HQ * DK * u, HQ * DK)]
                dve.tensor_tensor(dst.rearrange("p i (h c) -> p i h c", h=HQ), ps[:, :, :, 0:DK],
                                  rden[:, c, :, :].unsqueeze(3).broadcast_to([P, 4, HQ, DK]),
                                  ALU.mult).then_inc(s["aux_free"], 1)

            dve.wait_ge(s["const_ready"], 5)
            for k in range(NM):
                max_unit(k, k, k, 0)
            maxima(0, NM)
            for k in range(FIRST):
                max_unit(k, NM + k, NM + k, 1)
            neg_out(NM + FIRST, NM + FIRST)
            for k in range(FIRST, NM // 2):
                max_unit(k, NM + 1 + k, NM + 1 + k, 1)
            base = link[0]

            def body(t, u, p, plan):
                a = 0
                a0 = AUX0 + AUXN * t
                par = AUX0 + AUXN * p
                for q in TURN:
                    for kind, k, unit in [x for step in plan[q] for x in step]:
                        if kind == "max":
                            max_unit(unit, a0 + a, par + a, (p + k) % 2)
                        elif kind == "turn":
                            dve.wait_ge(s["negrow"], 16 * t + 16)
                            neg_out(a0 + a, par + a)
                        else:
                            attn_out(u, p, k, a0 + a, par + a, base + 2 * t + k)
                        a += 1
                    if q == 2:
                        dve.wait_ge(s["neg3_ready"], t + 1)
                        maxima(1 - p, a0 + a)
                return a

            with dve.Fori(0, T // 2 - 1) as u:
                for p in range(2):
                    body(2 * u + p, u, p, FULL)
            a = AUX0 + AUXN * (T - 2) + body(T - 2, T // 2 - 1, 0, NOT_AHEAD)
            for c in range(2):
                attn_out(T // 2 - 1, 1, c, a + c, a + c, base + 2 * (T - 1) + c)
            link[0] = base + 2 * T

            for g in range(4):
                dve.wait_ge(s["pj_ready"], g + 1)
                ins = dve.tensor_tensor(x_sb[:, 4 * g:4 * g + 4, :], oacc[:, g % 2, :].rearrange("p (n c) -> p n c", n=4),
                                        x_sb[:, 4 * g:4 * g + 4, :], ALU.add)
                ins.then_inc(s["x2_done"], 1)
            dve.wait_ge(s["x2_done"], 4)
            aggregate(list(range(NT)), s["var2_ready"])
            rstd(slice(0, NT), (s["std2_ready"], 1))
            for n in range(NT):
                normalise(n, s["xn2_ready"])
            dve.wait_ge(s["lg_ready"], 4)
            chained(dve.tensor_copy(lg[:, :, :], oacc[:, 1, 0:NT * NE].rearrange("p (n e) -> p n e", e=NE)))
            chained(dve.tensor_reduce(gmx[:, :], lg[:, :, :], AX_X, ALU.max))
            dve.tensor_tensor(lg[:, :, :], lg[:, :, :], gmx[:, :].unsqueeze(2).broadcast_to([P, NT, NE]),
                              ALU.subtract).then_inc(s["ge_ready"], 1)
            dve.wait_ge(s["gx_ready"], 1)
            chained(dve.tensor_reduce(gsm[:, :], gt[:, :, :], AX_X, ALU.add))
            chained(dve.reciprocal(gsm[:, :], gsm[:, :]))
            chained(dve.tensor_tensor(gt[:, :, :], gt[:, :, :], gsm[:, :].unsqueeze(2).broadcast_to([P, NT, NE]),
                                      ALU.mult))
            for n in range(NT):
                ins = dve.max(top[:, n, :], gt[:, n, :])
            chained(ins)
            for n in range(NT):
                ins = dve.max_index(topi[:, n, :], top[:, n, :], gt[:, n, :])
            chained(ins)
            dve.tensor_copy(topf[:, :, :], topi[:, :, 0:2])
            dve.tensor_tensor(tw[:, :, 0], top[:, :, 1], top[:, :, 0], ALU.subtract).then_inc(s["ge_ready"], 1)
            dve.wait_ge(s["gx_ready"], 2)
            chained(dve.tensor_scalar(tw[:, :, 0], tw[:, :, 1], 1.0, None, ALU.add))
            chained(dve.reciprocal(tw[:, :, 0], tw[:, :, 0]))
            chained(dve.tensor_tensor(tw[:, :, 1], tw[:, :, 1], tw[:, :, 0], ALU.mult))
            io = iota8[:, :].unsqueeze(1).broadcast_to([P, NT, NE])
            for k in range(2):
                dst = wsel[:, :, :] if k else wgt[:, :, 0:NE]
                chained(dve.tensor_tensor(dst, io, topf[:, :, k:k + 1].broadcast_to([P, NT, NE]), ALU.is_equal))
                chained(dve.tensor_tensor(dst, dst, tw[:, :, k:k + 1].broadcast_to([P, NT, NE]), ALU.mult))
            dve.tensor_tensor(wgt[:, :, 0:NE], wgt[:, :, 0:NE], wsel[:, :, :], ALU.add).then_inc(s["wgt_ready"], 1)
            for g in range(4):
                dve.wait_ge(s["wt_ready"], g + 1)
                dve.tensor_copy(wT[:, 512 * g:512 * g + 512], aux[0:NE + 1, g % 2, :]).then_inc(s["wT_ready"], 1)

            def down_bank(c):
                return oacc[:, c % 2, :].rearrange("p (n c) -> p n c", n=4)

            for c in range(STEPS):
                dve.wait_ge(s["dn_ready"], c + 1)
                dve.tensor_copy(acc[:, 4 * c:4 * c + 4, :], down_bank(c)).then_inc(s["acc_done"], 1)

            def expert(k0, p, last):
                for c in range(STEPS):
                    dve.wait_ge(s["acc_done"], k0 + c - 3)
                    dve.wait_ge(s["dn_ready"], k0 + c + 1)
                    for i in range(4):
                        n = 4 * c + i
                        ins = dve.scalar_tensor_tensor(out=acc[:, n, :], in0=down_bank(c)[:, i, :],
                                                       scalar=wcur[:, p, n:n + 1], in1=acc[:, n, :],
                                                       op0=ALU.mult, op1=ALU.add)
                    ins.then_inc(s["acc_done"], 1)
                    if last:
                        dve.wait_ge(s["acc_done"], k0 + c + 1)
                        tiles = slice(4 * c, 4 * c + 4)
                        gate = gB[:, 1, c // 2:c // 2 + 1, :].broadcast_to([P, 4, C])
                        chained(dve.tensor_tensor(acc[:, tiles, :], acc[:, tiles, :], gate, ALU.mult))
                        dve.tensor_tensor(yout[:, tiles, :], acc[:, tiles, :], x_sb[:, tiles, :],
                                          ALU.add).then_inc(s["y_ready"], 1)

            with dve.Fori(0, NE // 2 - 1) as u:
                for p in range(2):
                    e = 2 * u + p
                    dve.wait_ge(s["cur_ready"], e + 1)
                    expert(STEPS * (e + 1), p, False)
            for p in range(2):
                e = NE - 2 + p
                dve.wait_ge(s["cur_ready"], e + 1)
                expert(STEPS * (e + 1), p, p == 1)

        @block.tensor
        def _(pe):
            pe.sem_inc(s["pv_done"], 1)
            pe.sem_inc(s["out_turned"], 2)
            pe.wait_ge(s["w_in"], 128)
            for k in range(3):
                ins = pe.matmul(aux[:, 0, P * k:P * k + P], wd_sb[:, min(k, 1), :], wu_sb[:, k, :],
                                start=True, stop=True)
            ins.then_inc(s["comp_ready"], 1)
            pe.wait_ge(s["cs_ready"], 1)
            for j in range(6):
                pe.matmul(aux[:, 1, 2 * j:2 * j + 2], wmod_sb[:, C * j:C * j + C], cs[:, :], start=True, stop=True)
            pe.wait_ge(s["csb_ready"], 1)
            for k in range(2):
                for b in range(B):
                    ins = pe.matmul(oacc[:, 0, P * (2 * k + b):P * (2 * k + b) + P], csB[:, b, :],
                                    wmod_sb[:, C * (3 * k + 2):C * (3 * k + 3)], start=True, stop=True)
            ins.then_inc(s["mod_ready"], 1)
            pe.wait_ge(s["const_ready"], 2)

            def x_turn(g):
                if g >= 2:
                    pe.wait_ge(s["hT_ready"], g - 1)
                for i in range(4):
                    n = 4 * g + i
                    pe.wait_ge(s["xn_ready"], n + 1)
                    ins = pe.transpose(sc[:, g % 2, P * i:P * i + P], xn[:, n, :], ident[:, :])
                ins.then_inc(s["xT_ready"], 1)

            def project(n):
                b, kq, half = QK[n]
                pe.wait_ge(s["hT_ready"], 2 * b + half + 1)
                if n >= 3:
                    pe.wait_ge(s["r1_ready"], n - 2)
                pe.matmul(qk_bank[n % 3], wqkv[:, 1 - kq, :], hT[:, b * S + 512 * half:b * S + 512 * half + 512],
                          start=True, stop=True).then_inc(s["qk_ready"], 1)

            def project_v(g):
                if g >= 2:
                    pe.wait_ge(s["v_done"], g - 1)
                elif g == 1:
                    pe.wait_ge(s["mod_done"], 1)
                for i in range(4):
                    n = 4 * g + i
                    ins = pe.matmul(aux[:, g % 2, P * i:P * i + P], hT[:, P * n:P * n + P], wqkv[:, 2, :],
                                    start=True, stop=True)
                ins.then_inc(s["v_ready"], 1)

            x_turn(0)
            x_turn(1)
            pe.wait_ge(s["wqkv_ready"], 1)
            for n in range(4):
                project(n)
            project_v(0)
            project_v(1)
            x_turn(2)
            x_turn(3)
            for n in range(4, 8):
                project(n)
            project_v(2)
            project_v(3)

            def max_scores(k, a, par, p):
                h, i, k0, w, diagonal, place = MAXU[k]
                if not isinstance(a, int) or a >= 2:
                    pe.wait_ge(s["aux_free"], a - 1)
                pe.matmul(aux[:, par % 2, 0:w], S1[0:CROSS, p, 1, S * h + P * i:S * h + P * i + P],
                          S1[0:CROSS, p, 0, S * h + k0:S * h + k0 + w], start=True, stop=True).then_inc(s["aux_ready"], 1)

            def turn_max(a, par, n):
                pe.wait_ge(s["neg3_ready"], n)
                pe.wait_ge(s["aux_free"], a - 1)
                pe.transpose(aux[0:96, par % 2, 0:64].bitcast(BF16), neg3[:, :, :].rearrange("p a c -> p (a c)"),
                             identb[:, :]).then_inc(s["aux_ready"], 1)

            def score_unit(t, slot, n, p):
                j, h0, nh, w, pitch = UNITS[slot][n]
                g = NU * t + UBASE[slot] + n
                if not isinstance(g, int) or g >= 2:
                    pe.wait_ge(s["exp_done"], g - 1)
                if slot == 0 and n == 0:
                    pe.wait_ge(s["negrow"], 16 * t + 16)
                buf = (UBASE[slot] + n) % 2
                dst = sc[:, 2 * buf:2 * buf + 2, :].rearrange("p a c -> p (a c)")
                for k in range(nh):
                    h = h0 + k
                    for c in range(0, w, 512):
                        m = min(512, w - c)
                        q = S * h + P * j + c
                        pe.matmul(dst[:, pitch * k + c:pitch * k + c + m],
                                  S2[0:NEG_ROW + 3, p, 0, S * h + P * j:S * h + P * j + P],
                                  S2[0:NEG_ROW + 3, p, 1, q:q + m], start=True, stop=True)
                    ins = pe.matmul(dst[:, pitch * k:pitch * k + P], identb[:, :], after[:, :],
                                    start=False, stop=True, skip_group_check=True)
                ins.then_inc(s["score_ready"], 1)

            def weigh(t, slot, c, p):
                j = SLOTS[slot]
                q0 = max(512 * c, P * j)
                if c == 0 or slot % 2:
                    pe.wait_ge(s["exp_done"], NU * t + UBASE[slot + 1])
                if slot == 0 and c == 0:
                    pe.wait_ge(s["vb_ready"], t + 1)
                    pe.wait_ge(s["o_done"], 2 * t + 1)
                for h in range(HQ):
                    if slot % 2:
                        src = prs[:, h, q0 - 512:512]
                    else:
                        src = pr[:, slot // 2 % 2, h, q0:512 * c + 512]
                    ins = pe.matmul(oacc[VW * h:VW * h + VW, c, q0 - 512 * c:512], vb[:, p, j, h, :], src,
                                    start=(slot == 0), stop=(slot == (6 if c == 0 else 7)))
                if c == 1:
                    ins.then_inc(s["pv_done"], 1)

            def turn_out(t, c, a, par):
                pe.wait_ge(s["o_done"], 2 * t + c + 2)
                pe.wait_ge(s["aux_free"], a - 1)
                for i in range(4):
                    ins = pe.transpose(aux[:, par % 2, P * i:P * i + P], osb[:, c, P * i:P * i + P], ident[:, :])
                ins.then_inc(s["aux_ready"], 1)
                pe.sem_inc(s["out_turned"], 1)

            def weigh_pair(t, q, p, step):
                if step < 2:
                    weigh(t, 2 * q, step, p)
                if step == 1:
                    weigh(t, 2 * q + 1, 1, p)

            def body(t, u, p, plan, more):
                a = 0
                a0 = AUX0 + AUXN * t
                par = AUX0 + AUXN * p
                for q in TURN if more else (1, 2, 3):
                    at = (t + 1, 1 - p) if q == 0 else (t, p)
                    if q == 0:
                        pe.wait_ge(s2_in[1 - p], 32 * (u + p + 1))
                    if q == 3 and plan is FULL:
                        pe.wait_ge(s1_in[p], 16 * NLOAD * (u + 2))
                    for step, (slot, n) in enumerate(pair_steps(q)):
                        score_unit(at[0], slot, n, at[1])
                        weigh_pair(t, (q - 1) % 4, p, step)
                        for kind, k, unit in plan[q][step] if plan else ():
                            if kind == "max":
                                max_scores(unit, a0 + a, par + a, (p + k) % 2)
                            elif kind == "turn":
                                turn_max(a0 + a, par + a, t + 2)
                            else:
                                turn_out(t, k, a0 + a, par + a)
                            a += 1
                return a

            pe.wait_ge(s["v_done"], 4)
            pe.wait_ge(s1_in[0], 16 * NLOAD)
            for k in range(NM):
                max_scores(k, k, k, 0)
            pe.wait_ge(s1_in[1], 16 * NLOAD)
            for k in range(FIRST):
                max_scores(k, NM + k, NM + k, 1)
            turn_max(NM + FIRST, NM + FIRST, 1)
            for k in range(FIRST, NM // 4):
                max_scores(k, NM + 1 + k, NM + 1 + k, 1)
            pe.wait_ge(s2_in[0], 32)
            pe.wait_ge(s["r1_ready"], 8)
            steps = len(pair_steps(0))
            for step, (slot, n) in enumerate(pair_steps(0)):
                score_unit(0, slot, n, 0)
                for k in range(NM // 4 + NM // 4 * step // steps, NM // 4 + NM // 4 * (step + 1) // steps):
                    max_scores(k, NM + 1 + k, NM + 1 + k, 1)
            with pe.Fori(0, T // 2 - 1) as u:
                for p in range(2):
                    body(2 * u + p, u, p, FULL, True)
            a = AUX0 + AUXN * (T - 2) + body(T - 2, T // 2 - 1, 0, NOT_AHEAD, True)
            body(T - 1, T // 2 - 1, 1, None, False)
            for step in range(2):
                weigh_pair(T - 1, 3, 1, step)
            for c in range(2):
                turn_out(T - 1, c, a + c, a + c)

            pe.wait_ge(s["exp_done"], NU * T)
            pe.wait_ge(s["aux_free"], a + 2)
            pe.wait_ge(s["wog_ready"], 1)
            for g in range(5):
                if g < 4:
                    for i in range(4):
                        n = 4 * g + i
                        ins = pe.transpose(sc[:, g, P * i:P * i + P], attn[:, n, :],
                                           ident[:, :])
                    ins.then_inc(s["at_ready"], 1)
                if g:
                    k = g - 1
                    pe.wait_ge(s["at_done"], k + 1)
                    if k >= 2:
                        pe.wait_ge(s["x2_done"], k - 1)
                    else:
                        pe.wait_ge(s["o_done"], 2 * T + 1)
                    for i in range(4):
                        ins = pe.matmul(oacc[:, k % 2, P * i:P * i + P], aT[:, k % 2, P * i:P * i + P], wog[:, k // 2, :],
                                        start=True, stop=True)
                    ins.then_inc(s["pj_ready"], 1)
            pe.wait_ge(s["w2_in"], 16 * 9)
            for g in range(4):
                for i in range(4):
                    n = 4 * g + i
                    pe.wait_ge(s["xn2_ready"], n + 1)
                    ins = pe.transpose(sc[:, g, P * i:P * i + P], xn[:, n, :], ident[:, :])
                ins.then_inc(s["x2T_ready"], 1)
            for g in range(4):
                pe.wait_ge(s["h2T_ready"], g + 1)
                if g >= 2:
                    pe.wait_ge(s["r1T_ready"], g - 1)
                pe.matmul(aux[0:32, g % 2, :], wr1_sb[:, :], h2T[:, 512 * g:512 * g + 512],
                          start=True, stop=True).then_inc(s["rt_ready"], 1)
            for g in range(4):
                pe.wait_ge(s["r1T_ready"], g + 1)
                for i in range(4):
                    n = 4 * g + i
                    ins = pe.matmul(oacc[:, 1, NE * n:NE * n + NE], r1T[:, P * n:P * n + P], wr2_sb[:, :],
                                    start=True, stop=True)
                ins.then_inc(s["lg_ready"], 1)

            def up(k, c, w):
                for f in range(NF):
                    if not isinstance(k, int) or k >= 1:
                        pe.wait_ge(s["silu_done"], NF * k + f - NF + 1)
                    pe.matmul(sc[:, f, :], w[:, P * f:P * f + P], h2T[:, 512 * c:512 * c + 512],
                              start=True, stop=True).then_inc(s["up_ready"], 1)

            def down(k, c, w, shared):
                pe.wait_ge(s["silu_done"], NF * k + NF)
                if not isinstance(k, int) or k >= 2:
                    pe.wait_ge(s["acc_done"], k - 1)
                for i in range(4):
                    n = 4 * c + i
                    dst = oacc[:, c % 2, P * i:P * i + P]
                    if shared:
                        pe.matmul(dst, wT[:, P * n:P * n + P], be2_sb[:, :], start=True, stop=False)
                    for f in range(NF):
                        ins = pe.matmul(dst, sT[:, c % 2, f, P * i:P * i + P], w[:, f, :],
                                        start=(f == 0 and not shared), stop=(f == NF - 1))
                ins.then_inc(s["dn_ready"], 1)

            up(0, 0, sh_up[:, :])
            pe.wait_ge(s["wgt_ready"], 1)
            for g in range(4):
                if g >= 2:
                    pe.wait_ge(s["wT_ready"], g - 1)
                for i in range(4):
                    n = 4 * g + i
                    ins = pe.transpose(aux[0:NE + 1, g % 2, P * i:P * i + P], wgt[:, n, :], ident[:, :])
                ins.then_inc(s["wt_ready"], 1)
            for c in range(1, STEPS):
                up(c, c, sh_up[:, :])
                pe.wait_ge(s["wT_ready"], c)
                down(c - 1, c - 1, sh_dn[:, :, :], True)

            def first_up(k, p):
                up(k, 0, wup[:, p, :])

            pe.wait_ge(ew[0], 32)
            first_up(STEPS, 0)
            pe.wait_ge(s["wT_ready"], 4)
            down(3, 3, sh_dn[:, :, :], True)

            def rest(k0, p):
                for c in range(1, STEPS):
                    up(k0 + c, c, wup[:, p, :])
                    down(k0 + c - 1, c - 1, wdn[:, p, :, :], False)

            def finish(k0, p, count):
                pe.wait_ge(ew[1 - p], count)
                first_up(k0 + STEPS, 1 - p)
                down(k0 + 3, 3, wdn[:, p, :, :], False)

            with pe.Fori(0, NE // 2 - 1) as u:
                for p in range(2):
                    k0 = STEPS * (2 * u + p + 1)
                    rest(k0, p)
                    finish(k0, p, 32 * (u + p + 1))
            k0 = STEPS * (NE - 1)
            rest(k0, 0)
            finish(k0, 0, 32 * (NE // 2))
            rest(k0 + STEPS, 1)
            down(k0 + STEPS + 3, 3, wdn[:, 1, :, :], False)


def kernel(**inputs):
    import numpy as _np
    import concourse.bacc as _bacc
    from concourse import mybir as _mybir
    from concourse.bass_utils import run_bass_kernel_spmd as _run

    a = {k.replace("L0_", ""): _np.asarray(v) for k, v in inputs.items()}
    row = lambda v: v.reshape(1, -1)
    NE, F = a["ffn_be1"].shape
    biases = _np.concatenate([a["ffn_be1"], row(a["ffn_bs1"])], 0).reshape(NE + 1, F // 128, 128)
    data = {
        "x": a["attn_x"], "cT": a["c"].T, "wmod": a["wmod"], "wdqT": a["attn_W_dq"].T, "wdkvT": a["attn_W_dkv"].T,
        "wuq": a["attn_W_uq"], "wuk": a["attn_W_uk"], "wuv": a["attn_W_uv"], "wo": a["attn_W_o"],
        "wr1": a["ffn_Wr1"], "br1": a["ffn_br1"].reshape(-1, 1), "wr2": a["ffn_Wr2"], "br2": row(a["ffn_br2"]),
        "ws1": a["ffn_Ws1"], "ws2": a["ffn_Ws2"], "bs2": row(a["ffn_bs2"]), "we1": a["ffn_We1"], "we2": a["ffn_We2"],
        "be2": a["ffn_be2"], "b1T": biases.transpose(2, 0, 1).reshape(128, -1),
    }
    nc = _bacc.Bacc("TRN2", target_bir_lowering=False, num_devices=1)
    arrays, args = {}, []
    for name, v in data.items():
        v = _np.ascontiguousarray(v)
        arrays[f"in_{name}"] = v
        args.append(nc.dram_tensor(f"in_{name}", v.shape, _mybir.dt.from_np(v.dtype), kind="ExternalInput").ap())
    out = nc.dram_tensor("out_y", a["attn_x"].shape, _mybir.dt.float32, kind="ExternalOutput").ap()
    adaln_layer(nc, *args, out)
    r = _run(nc, [arrays], core_ids=[0])
    return r.results[0]["out_y"]
```

```python
from contextlib import ExitStack

import concourse.bass as bass
from concourse import mybir

ALU = mybir.AluOpType
ACT = mybir.ActivationFunctionType
AX_X = mybir.AxisListType.X
F32 = mybir.dt.float32
BF16 = mybir.dt.bfloat16
U32 = mybir.dt.uint32
I32 = mybir.dt.int32

P = 128
LOWEST = -3.0e38
EPS = 1e-5

SLOTS = [0, 7, 1, 6, 2, 5, 3, 4]
HQ = 4
DK = 8
VW = 32
NEG_ROW = 96
CROSS = 72


def score_units():
    out = []
    for j in SLOTS:
        w = 1024 - P * j
        n = 1 if w > 512 else (2 if w > 256 else 4)
        pitch = 1024 // n if w > 256 or n == 1 else w
        out.append([(j, h, n, w, pitch) for h in range(0, HQ, n)])
    return out


def max_units():
    out = []
    for i in range(8):
        w = P * (i + 1)
        if w > 512:
            out += [(i, 0, 512, False, 0), (i, 512, w - 512, True, 1)]
        else:
            out.append((i, 0, w, True, 0))
    return out


def pair_steps(q):
    units = score_units()
    return [(slot, n) for slot in (2 * q, 2 * q + 1) for n in range(len(units[slot]))]


TURN = (1, 2, 3, 0)


def aux_plan(nm, more, ahead):
    plan = {}
    for q in TURN:
        steps = len(pair_steps(q))
        units = []
        if q in (1, 2) and more:
            units = [("max", 1, nm // 2 + (q - 1) * nm // 4 + k) for k in range(nm // 4)]
        if q in (3, 0) and ahead:
            units = [("max", 2, (0 if q == 3 else nm // 4) + k) for k in range(nm // 4)]
        share = SHARES[q]
        cuts = [min(sum(share[:i]), len(units)) for i in range(steps + 1)]
        plan[q] = [units[cuts[i]:cuts[i + 1]] for i in range(steps)]
    if more:
        plan[3][TURN_STEP].append(("turn", 0, 0))
        plan[0][3].append(("out", 0, 0))
        plan[0][4].append(("out", 1, 0))
    return plan


SHARES = {0: (3, 3, 2, 2, 2), 1: (3, 3, 2, 2, 2), 2: (2, 2, 2, 2, 2, 2), 3: (2, 2, 2, 2, 2, 2)}
BEFORE = 2
TURN_STEP = 3


def adaln_layer(nc, x, cT, wmod, wdqT, wdkvT, wuq, wuk, wuv, wo, wr1, br1, wr2, br2,
                ws1, ws2, bs2, we1, we2, be2, b1T, out):
    B, S, C = x.shape
    assert (B, S, C) == (2, 1024, 128)
    NT = B * S // P
    NE = we1.shape[0]
    FF = ws1.shape[1]
    NF = FF // P
    NQ = 16 // HQ
    T = B * NQ
    UNITS = score_units()
    NU = sum(len(u) for u in UNITS)
    UBASE = [sum(len(u) for u in UNITS[:s]) for s in range(9)]
    MAXU = [(h, *m) for h in range(HQ) for m in max_units()]
    NM = len(MAXU)
    AUX0 = NM + NM // 2 + 1
    AUXN = NM + 3
    FULL = aux_plan(NM, True, True)
    NOT_AHEAD = aux_plan(NM, True, False)
    TURNED = NM // 2 + sum(len(x) for x in FULL[3][:TURN_STEP]) + len(FULL[3][TURN_STEP]) - 1
    FIRST = 4
    NLOAD = 12
    STEPS = 4
    FIRST_STEPS = 3
    TOK = B * S
    ROUTED = (2 * TOK + NE * (P - 1)) // P + 1
    ROWS = 8
    assert ROUTED % ROWS == 0
    FREE = 4

    with ExitStack() as ctx:
        def sb(name, shape, dt):
            return ctx.enter_context(nc.sbuf_tensor(name, shape, dt))

        def sem(name):
            return ctx.enter_context(nc.semaphore(name))

        sc = ctx.enter_context(nc.psum_tensor("sc", [P, 4, 512], F32))
        aux = ctx.enter_context(nc.psum_tensor("aux", [P, 2, 512], F32))
        oacc = ctx.enter_context(nc.psum_tensor("oacc", [P, 2, 512], F32))

        x_sb = sb("x_sb", [P, NT, C], F32)
        cT_sb = sb("cT_sb", [P, B], F32)
        cs = sb("cs", [P, B], F32)
        csB = sb("csB", [P, B, P], F32)
        wmod_sb = sb("wmod_sb", [P, 6 * C], F32)
        wd_sb = sb("wd_sb", [32, 2, C], F32)
        wu_sb = sb("wu_sb", [32, 3, C], F32)
        wo_sb = sb("wo_sb", [P, C], F32)
        wr1_sb = sb("wr1_sb", [P, 32], F32)
        br1_sb = sb("br1_sb", [32, 1], F32)
        wr2_sb = sb("wr2_sb", [33, NE], F32)
        be2_sb = sb("be2_sb", [NE + 1, C], F32)
        b1_sb = sb("b1_sb", [P, (NE + 1) * NF], F32)
        ident = sb("ident", [P, P], F32)
        identb = sb("identb", [P, P], BF16)
        after = sb("after", [P, P], BF16)
        slab = sb("slab", [P, 512], F32)
        iota8 = sb("iota8", [P, NE], F32)
        wqkv = sb("wqkv", [P, 3, C], F32)
        modT = sb("modT", [P, 6, B], F32)
        scl = sb("scl", [P, 2, B], F32)
        gB = sb("gB", [P, 2, B, C], F32)
        wog = sb("wog", [P, B, C], F32)
        stats = sb("stats", [P, NT, 6], F32)
        mv = sb("mv", [P, NT, 2], F32)
        var = sb("var", [P, NT], F32)
        std = sb("std", [P, NT], F32)
        rst = sb("rst", [P, NT], F32)
        nwt = sb("nwt", [P, NT], F32)
        hT = sb("hT", [P, NT * P], F32)
        parts = sb("parts", [P, 2, 3, NT * P], BF16)
        valt = sb("valt", [P, NT, C], F32)
        S1 = sb("S1", [P, 2, 2, HQ * S], BF16)
        S2 = sb("S2", [P, 2, 2, HQ * S], BF16)
        vb = sb("vb", [P, 2, 8, HQ, VW], F32)
        pr = sb("pr", [P, 2, HQ, S], F32)
        prs = sb("prs", [P, HQ, 512], F32)
        mxp = sb("mxp", [P, 2, HQ * 8, 2], F32)
        negm = sb("negm", [P, HQ * 8], F32)
        negr = sb("negr", [P, HQ * 8], F32)
        gsgn, gabs = (pr[:, 0, k, 0:2 * B * C].rearrange("p (k b c) -> p k b c", k=2, b=B) for k in range(2))
        neg3 = sb("neg3", [P, 3, HQ * 8], BF16)
        negT = sb("negT", [96, P], BF16)
        osb = sb("osb", [P, 2, 512], F32)
        r1 = osb
        rden = sb("rden", [P, 2, 4, HQ], F32)
        attn = sb("attn", [P, NT, C], F32)
        xn = attn
        aT = hT[:, 0:1024].rearrange("p (a n) -> p a n", a=2)
        sT = pr
        weights = S1[:, :, :, :].rearrange("p a b n -> p (a b n)").bitcast(F32).rearrange("p (e n) -> p e n", e=NE)
        late = S2[:, :, :, :].rearrange("p a b n -> p (a b n)").bitcast(F32)
        yk = late[:, 0:2 * NT * C].rearrange("p (k n c) -> p k n c", k=2, c=C)
        onehot = late[:, 0:NT * C].bitcast(BF16).rearrange("p (k n b) -> p k n b", k=2, n=NT)
        acc = late[:, 4096:4096 + NT * C].rearrange("p (n c) -> p n c", c=C)
        yst = late[:, 6144:6144 + ROWS * C].rearrange("p (n c) -> p n c", c=C)
        xrow = late[:, 7168:7168 + FREE * C].rearrange("p (n c) -> p n c", c=C)
        xTg = late[:, 7680:7680 + 2 * C].rearrange("p (n c) -> p n c", c=C)
        yout = attn
        wT = valt[0:NE + 1, :, :].rearrange("p n c -> p (n c)")
        free = parts[:, :, :, :].rearrange("p a b n -> p (a b n)")
        rows = free[:, 0:2 * NT * C].bitcast(F32).rearrange("p (n c) -> p n c", n=NT)
        tiled, tiledp, tiledn = (free[:, 4096 + 1280 * k:4096 + 1280 * (k + 1)].rearrange(
            "p (k n a) -> p k n a", k=2, n=NT) for k in range(3))
        tiledpn = free[:, 4096 + 1280:4096 + 3 * 1280].rearrange("p (q k n a) -> p q k n a", q=2, k=2, n=NT)
        wcur = vb[:, :, :, :, :].rearrange("p a j h c -> p a (j h c)")
        hid = prs[:, 0:2, :]
        h2T = hT
        r1T = sb("r1T", [33, NT * P], F32)
        lg = sb("lg", [P, NT, NE], F32)
        gt = sb("gt", [P, NT, NE], F32)
        gmx = sb("gmx", [P, NT], F32)
        gsm = sb("gsm", [P, NT], F32)
        top = sb("top", [P, NT, 8], F32)
        topi = sb("topi", [P, NT, 8], U32)
        topf = sb("topf", [P, NT, 2], F32)
        tw = sb("tw", [P, NT, 2], F32)
        wgt = sb("wgt", [P, NT, NE + 1], F32)
        wsel = pr[:, 0, 0, 704:704 + NT * NE].rearrange("p (n e) -> p n e", e=NE)
        chosen = sb("chosen", [P, (NT + 1) * NE], BF16)
        upper = sb("upper", [P, P], BF16)
        ones = sb("ones", [P, P], BF16)
        thr = sb("thr", [P, NT], F32)
        lower = sb("lower", [P, NE, NE], F32)
        num = sb("num", [P, P], F32)
        pnum = sb("pnum", [P, 1], F32)
        posa = sb("posa", [P, 2, NT], F32)
        posm = sb("posm", [P, 2, NT], I32)
        posb = sb("posb", [P, 2, NT], F32)
        invn = sb("invn", [P, ROUTED], F32)
        inv = sb("inv", [P, ROUTED], I32)
        spare = pr[:, 0, :, 512:1024]
        isgt = spare[:, 0, 0:NE * NT].rearrange("p (e n) -> p e n", e=NE)
        tiles_e = sb("tiles_e", [P, NE], F32)
        before = spare[:, 0, 128:128 + NE * NE].rearrange("p (a e) -> p a e", e=NE)
        base_e = sb("base_e", [P, NE], F32)
        ends_e = sb("ends_e", [P, NE], F32)
        past = spare[:, 1, 0:ROUTED * NE].rearrange("p (n e) -> p n e", e=NE)
        tile_e = sb("tile_e", [P, ROUTED], F32)
        tile_i = sb("tile_i", [P, ROUTED], I32)
        place = spare[:, 2, 0:NT * NE].rearrange("p (n e) -> p n e", e=NE)
        place1 = spare[:, 3, 0:NT * NE].rearrange("p (n e) -> p n e", e=NE)
        posf = sb("posf", [P, 2, NT], F32)
        posi = sb("posi", [P, 2, NT], I32)
        icur = sb("icur", [P, FREE], I32)
        bcur = sb("bcur", [P, FREE, NF], F32)
        sh_up = sb("sh_up", [P, FF], F32)
        sh_dn = sb("sh_dn", [P, NF, C], F32)

        kd = nc.dram_tensor("k_parts", [T, HQ, 3, DK, S], BF16, kind="Internal").ap()
        qd = nc.dram_tensor("q_parts", [T, HQ, 3, DK, S], BF16, kind="Internal").ap()

        hd = nc.dram_tensor("hidden_rows", [TOK, C], F32, kind="Internal").ap()
        yd = nc.dram_tensor("sorted_results", [ROUTED * P, C], F32, kind="Internal").ap()

        names = """x_in0 x_in1 w_in w2_in parts_out0 parts_out1 s1_in0 s1_in1 s2_in0 s2_in1 negrow y_out y_done ew_in h2_out
            rows_in0 rows_in1 rows_in2 rows_in3 y_stored0 y_stored1 yk_in0 yk_in1 yk_in2 yk_in3
            chosen_ready prefix_ready rowmod_ready h2_ready onehot_ready tiled_ready numbered inv_sum
            inv_ready idx_ready te_ready xt_ready xt_done up_w down_w
            const_ready pad_ready chain_v chain_p chain_a cs_ready csb_ready comp_ready wqkv_ready mod_ready mod_done
            var_ready std_ready xn_ready xT_ready hT_ready qk_ready hi_ready r1_ready mid_ready lo_ready
            v_ready v_done aux_ready aux_free negm_ready neg3_ready score_ready exp_done
            vb_ready pv_done o_done out_turned at_ready at_done pj_ready x2_done var2_ready std2_ready
            xn2_ready x2T_ready h2T_ready rt_ready r1T_ready lg_ready ge_ready gx_ready gp_ready wgt_ready wt_ready
            wT_ready up_ready silu_done dn_ready acc_done y_ready wog_ready
            passed_v passed_s passed_p""".split()
        s = {n: sem(n) for n in names}
        x_in = [s["x_in0"], s["x_in1"]]
        parts_out = [s["parts_out0"], s["parts_out1"]]
        s1_in = [s["s1_in0"], s["s1_in1"]]
        s2_in = [s["s2_in0"], s["s2_in1"]]
        rows_in = [s[f"rows_in{k}"] for k in range(FREE)]
        y_stored = [s[f"y_stored{k}"] for k in range(2)]
        yk_in = [s[f"yk_in{k}"] for k in range(4)]

        block = ctx.enter_context(nc.Block())

        QK = [(b, kq, half) for b in range(B) for kq in range(2) for half in range(2)]
        qk_bank = [sc[:, 2, :], sc[:, 3, :], oacc[:, 1, :]]

        @block.sync
        def _(sp):
            xv = x.rearrange("b (n p) c -> b p n c", p=P)
            sp.dma_start(x_sb[:, 0:8, :], xv[0]).then_inc(x_in[0], 16)
            sp.dma_start(x_sb[:, 8:16, :], xv[1]).then_inc(x_in[1], 16)
            for dst, src in ((wr1_sb[:, :], wr1), (br1_sb[:, :], br1), (wr2_sb[0:32, :], wr2),
                             (wr2_sb[32:33, :], br2), (be2_sb[0:NE, :], be2), (be2_sb[NE:NE + 1, :], bs2),
                             (b1_sb[:, :], b1T), (sh_up[:, :], ws1),
                             (sh_dn[:, :, :], ws2.rearrange("(f p) c -> p f c", p=P))):
                sp.dma_start(dst, src).then_inc(s["w2_in"], 16)

            def store_parts(b):
                for kq, dst in ((0, kd), (1, qd)):
                    for part in range(3):
                        done = 4 * b + 2 * kq + 2
                        sp.wait_ge((s["hi_ready"], s["mid_ready"], s["lo_ready"])[part], done)
                        sp.dma_start(
                            dst[NQ * b:NQ * b + NQ, :, part, :, :].rearrange("t h d n -> (t h) d n"),
                            parts[:, kq, part, b * S:(b + 1) * S]).then_inc(parts_out[b], 16)

            def load_s1(u, p):
                sp.wait_ge(parts_out[p], 96)
                sp.sem_inc(s["passed_s"], 1)
                kt = kd[bass.ds(NQ * p + u, 1)].rearrange("t h a d n -> (t h) a d n")
                qt = qd[bass.ds(NQ * p + u, 1)].rearrange("t h a d n -> (t h) a d n")
                for a in range(3):
                    sp.dma_start(S1[24 * a:24 * a + 24, p, 0, :].rearrange("r (h n) -> r h n", h=HQ),
                                 kt.rearrange("h b d n -> (b d) h n")).then_inc(s1_in[p], 16)
                    for b in range(3):
                        r = 24 * a + 8 * b
                        sp.dma_start(S1[r:r + 8, p, 1, :].rearrange("r (h n) -> r h n", h=HQ),
                                     qt[:, a, :, :].rearrange("h d n -> d h n")).then_inc(s1_in[p], 16)

            def copy_s2(p):
                for kq in range(2):
                    sp.dma_start(S2[0:CROSS, p, kq, :], S1[0:CROSS, p, kq, :]).then_inc(s2_in[p], 16)

            def neg_rows(p):
                sp.dma_start(S2[NEG_ROW:NEG_ROW + 3, p, 1, :].rearrange("r (s q) -> r s q", q=P),
                             negT[:, :]).then_inc(s["negrow"], 16)

            store_parts(0)
            load_s1(0, 0)
            sp.wait_ge(s1_in[0], 16 * NLOAD)
            sp.wait_ge(s["pad_ready"], 1)
            copy_s2(0)
            store_parts(1)
            load_s1(0, 1)
            sp.wait_ge(s["aux_free"], NM + FIRST + 1)
            neg_rows(0)
            sp.wait_ge(s2_in[0], 32)
            load_s1(1, 0)

            def body(t, u, p, load, whole=True):
                sp.wait_ge(s1_in[1 - p], 16 * NLOAD * (u + p + 1))
                sp.sem_inc(s["passed_s"], 1)
                sp.wait_ge(s["score_ready"], NU * t + UBASE[2])
                copy_s2(1 - p)
                sp.wait_ge(s["aux_free"], AUX0 + AUXN * t + (TURNED if whole else NM // 2) + 1)
                neg_rows(1 - p)
                if load:
                    sp.wait_ge(s2_in[1 - p], 32 * (u + p + 1))
                    load_s1(u + 1 + p, 1 - p)

            with sp.Fori(0, T // 2 - 2) as u:
                for p in range(2):
                    body(2 * u + p, u, p, True)
            body(T - 4, T // 2 - 2, 0, True)
            body(T - 3, T // 2 - 2, 1, False)
            body(T - 2, T // 2 - 1, 0, False, whole=False)

            sp.wait_ge(s2_in[1], 32 * (T // 2))
            sp.dma_start(weights[:, :, 0:FF], we1.rearrange("e c f -> c e f")).then_inc(s["ew_in"], 16)
            for f in range(NF):
                sp.dma_start(weights[:, :, FF + C * f:FF + C * f + C],
                             we2.rearrange("e (f p) c -> f p e c", p=P)[f]).then_inc(s["ew_in"], 16)
            sp.wait_ge(s["h2_ready"], 1)
            sp.dma_start(hd.rearrange("(n p) c -> p n c", p=P), rows).then_inc(s["h2_out"], 16)
            G = ROWS // 2
            with sp.Fori(0, ROUTED // ROWS) as u:
                for k in range(2):
                    sp.wait_ge(s["y_done"], G * (2 * u + k) + G + 2)
                    sp.sem_inc(s["passed_s"], 1)
                    sp.dma_start(yd.rearrange("(n p) c -> p n c", p=P)[:, bass.ds(ROWS * u + G * k, G), :],
                                 yst[:, G * k:G * k + G, :]).then_inc(y_stored[k], 16)
            yv = out.rearrange("b (n p) c -> p (b n) c", p=P)
            for g in range(4):
                sp.wait_ge(s["y_ready"], g + 1)
                sp.dma_start(yv[:, 4 * g:4 * g + 4, :], yout[:, 4 * g:4 * g + 4, :]).then_inc(s["y_out"], 16)
            sp.wait_ge(s["y_out"], 64)

        @block.gpsimd
        def _(pool):
            link = [0]

            def chained(ins):
                link[0] += 1
                ins.then_inc(s["chain_p"], 1)
                pool.wait_ge(s["chain_p"], link[0])

            chained(pool.memset(ident[:, :], 0.0))
            chained(pool.affine_select(out=ident[:, :], in_=ident[:, :], compare_op=ALU.not_equal, fill=1.0,
                                       base=0, pattern=[[-1, P]], channel_multiplier=1))
            pool.tensor_copy(identb[:, :], ident[:, :]).then_inc(s["const_ready"], 1)
            chained(pool.memset(after[:, :], 0.0))
            pool.affine_select(out=after[:, :], in_=after[:, :], compare_op=ALU.is_ge, fill=LOWEST,
                               base=0, pattern=[[1, P]], channel_multiplier=-1).then_inc(s["const_ready"], 1)
            chained(pool.memset(slab[:, :], 0.0))
            pool.affine_select(out=slab[:, 384:512], in_=slab[:, 384:512], compare_op=ALU.is_ge, fill=LOWEST,
                               base=0, pattern=[[-1, P]], channel_multiplier=1).then_inc(s["const_ready"], 1)
            pool.memset(mxp[:, :, :, :], LOWEST).then_inc(s["const_ready"], 1)
            pool.iota(iota8[:, :], pattern=[[1, NE]], base=0, channel_multiplier=0,
                      allow_small_or_imprecise_dtypes=True).then_inc(s["const_ready"], 1)
            for k in range(2):
                pool.sem_inc(y_stored[k], 1)
            pool.wait_ge(s["const_ready"], 5)
            for p in range(2):
                chained(pool.memset(S2[64:128, p, :, :].bitcast(F32), 0.0))
                chained(pool.memset(S2[NEG_ROW:NEG_ROW + 3, p, 0, :], 1.0))
            pool.memset(r1T[32:33, :], 1.0).then_inc(s["pad_ready"], 1)
            pool.wait_ge(s["pad_ready"], 1)
            for n, (b, kq, half) in enumerate(QK):
                cols = slice(b * S + 512 * half, b * S + 512 * half + 512)
                pool.wait_ge(s["mid_ready"], n + 1)
                pool.tensor_tensor(parts[:, kq, 2, cols], r1[:, n % 2, :], parts[:, kq, 1, cols],
                                   ALU.subtract).then_inc(s["lo_ready"], 1)
                if n == 3:
                    chained(pool.memset(vb[:, :, :, :, :], 0.0))
                    chained(pool.memset(vb[:, :, :, :, DK:DK + 1], 1.0))
            chained(pool.memset(wgt[:, :, NE:NE + 1], 1.0))
            chained(pool.memset(ones[:, :], 1.0))
            chained(pool.memset(chosen[:, 0:NE], 0.0))
            chained(pool.memset(upper[:, :], 1.0))
            chained(pool.affine_select(out=upper[:, :], in_=upper[:, :], compare_op=ALU.is_ge, fill=0.0,
                                       base=-1, pattern=[[1, P]], channel_multiplier=-1))
            chained(pool.memset(lower[:, :, :], 1.0))
            chained(pool.affine_select(out=lower[:, :, :], in_=lower[:, :, :], compare_op=ALU.is_ge, fill=0.0,
                                       base=-1, pattern=[[1, NE], [-1, NE]], channel_multiplier=0))
            chained(pool.iota(thr[:, :], pattern=[[P, NT]], base=0, channel_multiplier=0,
                              allow_small_or_imprecise_dtypes=True))
            chained(pool.iota(num[:, :], pattern=[[1, P]], base=0, channel_multiplier=0,
                              allow_small_or_imprecise_dtypes=True))
            chained(pool.iota(pnum[:, :], pattern=[[0, 1]], base=0, channel_multiplier=1,
                              allow_small_or_imprecise_dtypes=True))

            def split_max(v):
                pool.sem_inc(s["passed_p"], 1)
                pool.tensor_copy(neg3[:, 0, :], negm[:, :]).then_inc(s["chain_p"], 1)
                pool.wait_ge(s["chain_p"], v + 1)
                pool.tensor_tensor(negr[:, :], negm[:, :], neg3[:, 0, :], ALU.subtract).then_inc(s["chain_p"], 1)
                pool.wait_ge(s["chain_p"], v + 2)
                pool.sem_inc(s["passed_p"], 1)
                pool.tensor_copy(neg3[:, 1, :], negr[:, :]).then_inc(s["chain_p"], 1)
                pool.wait_ge(s["chain_p"], v + 3)
                pool.tensor_tensor(neg3[:, 2, :], negr[:, :], neg3[:, 1, :], ALU.subtract).then_inc(s["neg3_ready"], 1)

            def values(u, p):
                pool.wait_ge(s["v_done"], 4)
                src = valt[:, 8 * p:8 * p + 8, bass.ds(HQ * DK * u, HQ * DK)]
                pool.tensor_copy(vb[:, p, :, :, 0:DK],
                                 src.rearrange("p j (h d) -> p j h d", h=HQ)).then_inc(s["vb_ready"], 1)

            base = link[0]
            values(0, 0)
            pool.wait_ge(s["negm_ready"], 1)
            split_max(base)

            def body(t, u, p):
                pool.wait_ge(s["pv_done"], 8 * t + 1)
                values(u + p, 1 - p)
                pool.wait_ge(s["negm_ready"], t + 2)
                split_max(base + 3 * t + 3)

            with pool.Fori(0, T // 2 - 1) as u:
                for p in range(2):
                    body(2 * u + p, u, p)
            body(T - 2, T // 2 - 1, 0)

            pool.wait_ge(s["tiled_ready"], 1)
            pool.tensor_scalar(tiledp, tiled, pnum[:, 0:1], None, ALU.mult).then_inc(s["tiled_ready"], 1)
            pool.wait_ge(s["tiled_ready"], 2)
            pool.tensor_tensor(tiledn, tiled, num[:, 0:NT].unsqueeze(1).unsqueeze(3).broadcast_to([P, 2, NT, ROUTED]),
                               ALU.mult).then_inc(s["tiled_ready"], 1)

            def gather_tile(i, j):
                pool.wait_ge(s["xt_ready"], i + 1)
                pool.sem_inc(s["passed_p"], 1)
                pool.tensor_copy(icur[:, j:j + 1], inv[:, bass.ds(i, 1)]).then_inc(s["idx_ready"], 1)
                pool.wait_ge(s["idx_ready"], i + 1)
                pool.sem_inc(s["passed_p"], 1)
                pool.indirect_dma_start(xrow[:, j, :], None, hd,
                                        bass.IndirectOffsetOnAxis(ap=icur[:, j:j + 1], axis=0)).then_inc(rows_in[j], 16)

            pool.wait_ge(s["inv_ready"], 1)
            pool.wait_ge(s["h2_out"], 16)
            with pool.Fori(0, ROUTED // FREE) as u:
                for j in range(FREE):
                    gather_tile(FREE * u + j, j)
            for k in range(2):
                pool.wait_ge(y_stored[k], 16 * (ROUTED // ROWS) + 1)
            for n in range(NT):
                for k in range(2):
                    pool.indirect_dma_start(yk[:, k, n, :], None, yd,
                                            bass.IndirectOffsetOnAxis(ap=posi[:, k, n:n + 1], axis=0)
                                            ).then_inc(yk_in[n // 4], 16)

        @block.scalar
        def _(act):
            act.sem_inc(s["o_done"], 1)
            act.sem_inc(s["y_done"], 2)
            for dst, src in ((cT_sb[:, :], cT), (wmod_sb[:, :], wmod), (wd_sb[:, 0, :], wdqT), (wd_sb[:, 1, :], wdkvT),
                             (wu_sb[:, 0, :], wuq), (wu_sb[:, 1, :], wuk), (wu_sb[:, 2, :], wuv), (wo_sb[:, :], wo)):
                act.dma_start(dst, src).then_inc(s["w_in"], 16)
            act.wait_ge(s["w_in"], 128)
            act.activation(cs[:, :], cT_sb[:, :], ACT.Silu).then_inc(s["cs_ready"], 1)

            def root(b):
                act.wait_ge(s["var_ready"], b + 1)
                act.activation(std[:, 8 * b:8 * b + 8], var[:, 8 * b:8 * b + 8], ACT.Sqrt).then_inc(s["std_ready"], 1)

            def h_out(g):
                act.wait_ge(s["xT_ready"], g + 1)
                if g == 0:
                    act.wait_ge(s["mod_done"], 1)
                act.activation(hT[:, 512 * g:512 * g + 512], sc[:, g % 2, :], ACT.Identity,
                               bias=modT[:, 0, g // 2:g // 2 + 1],
                               scale=scl[:, 0, g // 2:g // 2 + 1]).then_inc(s["hT_ready"], 1)

            def hi(n):
                b, kq, half = QK[n]
                act.wait_ge(s["qk_ready"], n + 1)
                act.activation(parts[:, kq, 0, b * S + 512 * half:b * S + 512 * half + 512], qk_bank[n % 3],
                               ACT.Copy).then_inc(s["hi_ready"], 1)

            def mid(n):
                b, kq, half = QK[n]
                act.wait_ge(s["r1_ready"], n + 1)
                act.activation(parts[:, kq, 1, b * S + 512 * half:b * S + 512 * half + 512], r1[:, n % 2, :],
                               ACT.Copy).then_inc(s["mid_ready"], 1)

            def v_out(g):
                act.wait_ge(s["v_ready"], g + 1)
                act.activation(
                    valt[:, 4 * g:4 * g + 4, :], aux[:, g % 2, :].rearrange("p (n c) -> p n c", n=4),
                    ACT.Copy).then_inc(s["v_done"], 1)

            for b in range(B):
                root(b)
                h_out(2 * b)
                h_out(2 * b + 1)
                for k in range(4):
                    hi(4 * b + k)
                    if k:
                        mid(4 * b + k - 1)
                mid(4 * b + 3)
                v_out(2 * b)
                v_out(2 * b + 1)

            def exps(t, q, steps):
                for slot, n in steps:
                    j, h, nh, w, pitch = UNITS[slot][n]
                    g = NU * t + UBASE[slot] + n
                    if n == 0:
                        used = 8 * t + (2 * q + 1 if slot % 2 else 2 * q - 2)
                        if not isinstance(t, int) or used > 1:
                            act.wait_ge(s["pv_done"], used)
                    act.wait_ge(s["score_ready"], g + 1)
                    buf = (UBASE[slot] + n) % 2
                    src = sc[:, 2 * buf:2 * buf + 2, :].rearrange("p a c -> p (a c)")
                    src = src[:, 0:nh * pitch].rearrange("p (h c) -> p h c", h=nh)[:, :, 0:w]
                    if slot % 2:
                        dst = prs[:, h:h + nh, P * j - 512:P * j - 512 + w]
                    else:
                        dst = pr[:, q % 2, h:h + nh, P * j:P * j + w]
                    act.activation(dst, src, ACT.Exp, scale=float(DK) ** -0.5).then_inc(s["exp_done"], 1)

            def o_out(t, c):
                act.wait_ge(s["pv_done"], 8 * t + 8 + c)
                if not isinstance(t, int) or t >= 1:
                    act.wait_ge(s["out_turned"], 2 * t + 1 + c)
                act.activation(osb[:, c, :], oacc[:, c, :], ACT.Copy).then_inc(s["o_done"], 1)

            exps(0, 0, pair_steps(0))

            def body(t, last=False):
                for q in (1, 2, 3):
                    exps(t, q, pair_steps(q))
                if not last:
                    exps(t + 1, 0, pair_steps(0)[0:2])
                o_out(t, 0)
                if not last:
                    exps(t + 1, 0, pair_steps(0)[2:3])
                o_out(t, 1)
                if not last:
                    exps(t + 1, 0, pair_steps(0)[3:])

            with act.Fori(0, T // 2 - 1) as u:
                for p in range(2):
                    body(2 * u + p)
            body(T - 2)
            body(T - 1, last=True)

            for g in range(4):
                act.wait_ge(s["at_ready"], g + 1)
                if g >= 2:
                    act.wait_ge(s["pj_ready"], g - 1)
                act.activation(aT[:, g % 2, :], sc[:, g, :], ACT.Copy).then_inc(s["at_done"], 1)
            act.wait_ge(s["var2_ready"], 1)
            act.activation(std[:, :], var[:, :], ACT.Sqrt).then_inc(s["std2_ready"], 1)
            for g in range(4):
                act.wait_ge(s["x2T_ready"], g + 1)
                act.activation(h2T[:, 512 * g:512 * g + 512], sc[:, g, :], ACT.Identity,
                               bias=modT[:, 3, g // 2:g // 2 + 1],
                               scale=scl[:, 1, g // 2:g // 2 + 1]).then_inc(s["h2T_ready"], 1)
                act.wait_ge(s["rt_ready"], g + 1)
                act.activation(r1T[0:32, 512 * g:512 * g + 512], oacc[0:32, g % 2, :], ACT.Relu,
                               bias=br1_sb[:, 0:1]).then_inc(s["r1T_ready"], 1)
            act.wait_ge(s["ge_ready"], 1)
            act.activation(gt[:, :, :], lg[:, :, :], ACT.Exp).then_inc(s["gx_ready"], 1)
            act.wait_ge(s["ge_ready"], 2)
            act.activation(tw[:, :, 1], tw[:, :, 0], ACT.Exp, scale=0.5).then_inc(s["gx_ready"], 1)

            def silu(k, c, bias, up_count=None):
                for f in range(NF):
                    act.wait_ge(s["up_ready"], (NF * k if up_count is None else up_count) + f + 1)
                    if f == 0 and (not isinstance(k, int) or k >= 2):
                        act.wait_ge(s["dn_ready"], k - 1)
                    act.activation(sT[:, c % 2, f, 0:512], sc[:, f, :], ACT.Silu,
                                   bias=bias[:, f:f + 1]).then_inc(s["silu_done"], 1)

            act.wait_ge(s["w2_in"], 16 * 9)
            for c in range(FIRST_STEPS):
                silu(c, c, b1_sb[:, NF * NE:NF * NE + NF])
            def silu_tile(i, j):
                act.wait_ge(s["up_ready"], NF * FIRST_STEPS + i + 1)
                act.wait_ge(s["dn_ready"], FIRST_STEPS + i - 1)
                for f in range(NF):
                    ins = act.activation(hid[:, j % 2, P * f:P * f + P], sc[:, j % 2, P * f:P * f + P], ACT.Silu,
                                         bias=bcur[:, j % FREE, f:f + 1])
                ins.then_inc(s["silu_done"], 1)

            def y_copy(i, j, u):
                act.wait_ge(s["dn_ready"], FIRST_STEPS + i + 1)
                if j % G == 0:
                    act.wait_ge(y_stored[j // G], 16 * u + 1)
                act.activation(yst[:, j, :], oacc[:, j % 2, 0:P], ACT.Copy).then_inc(s["y_done"], 1)

            G = ROWS // 2
            silu_tile(0, 0)
            with act.Fori(0, ROUTED // ROWS - 1) as u:
                for j in range(ROWS):
                    silu_tile(ROWS * u + j + 1, j + 1)
                    y_copy(ROWS * u + j, j, u)
            for j in range(ROWS):
                i = ROUTED - ROWS + j
                if i + 1 < ROUTED:
                    silu_tile(i + 1, j + 1)
                y_copy(i, j, ROUTED // ROWS - 1)
            silu(FIRST_STEPS + ROUTED, 3, b1_sb[:, NF * NE:NF * NE + NF], up_count=NF * FIRST_STEPS + ROUTED)

        @block.vector
        def _(dve):
            link = [0]

            def chained(ins):
                link[0] += 1
                ins.then_inc(s["chain_v"], 1)
                dve.wait_ge(s["chain_v"], link[0])

            def tile_stats(n):
                dve.bn_stats(stats[:, n, :], x_sb[:, n, :])

            def rstd(ns, wait):
                dve.wait_ge(*wait)
                chained(dve.reciprocal(rst[:, ns], std[:, ns]))
                chained(dve.tensor_tensor(nwt[:, ns], rst[:, ns], rst[:, ns], ALU.mult))
                chained(dve.tensor_tensor(nwt[:, ns], nwt[:, ns], var[:, ns], ALU.mult))
                chained(dve.tensor_scalar(nwt[:, ns], nwt[:, ns], -0.5, 1.5, ALU.mult, ALU.add))
                chained(dve.tensor_tensor(rst[:, ns], rst[:, ns], nwt[:, ns], ALU.mult))

            def aggregate(ns, done):
                ins = None
                for n in ns:
                    ins = dve.bn_stats(stats[:, n, :], x_sb[:, n, :])
                chained(ins)
                for n in ns:
                    ins = dve.bn_aggr(mv[:, n, :], stats[:, n, :])
                chained(ins)
                dve.tensor_scalar(var[:, ns[0]:ns[-1] + 1], mv[:, ns[0]:ns[-1] + 1, 1], EPS, None,
                                  ALU.add).then_inc(done, 1)

            def normalise(n, done):
                dve.tensor_scalar(xn[:, n, :], x_sb[:, n, :], mv[:, n, 0:1], rst[:, n:n + 1], ALU.subtract,
                                  ALU.mult).then_inc(done, 1)

            dve.wait_ge(x_in[0], 16)
            aggregate(list(range(8)), s["var_ready"])
            dve.wait_ge(s["cs_ready"], 1)
            for b in range(B):
                ins = dve.tensor_copy(csB[:, b, :], cs[:, b:b + 1].broadcast_to([P, P]))
            ins.then_inc(s["csb_ready"], 1)
            dve.wait_ge(s["comp_ready"], 1)
            dve.tensor_copy(wqkv[:, :, :], aux[:, 0, 0:384].rearrange("p (a c) -> p a c", a=3)).then_inc(s["wqkv_ready"], 1)
            rstd(slice(0, 8), (s["std_ready"], 1))
            for n in range(8):
                normalise(n, s["xn_ready"])
            dve.wait_ge(s["mod_ready"], 1)
            chained(dve.tensor_copy(modT[:, :, :], aux[:, 1, 0:12].rearrange("p (j b) -> p j b", b=B)))
            for k in range(2):
                ins = dve.tensor_scalar(scl[:, k, :], modT[:, 3 * k + 1, :], 1.0, None, ALU.add)
            ins.then_inc(s["mod_done"], 1)
            gps = oacc[:, 0, :].rearrange("p (k b c) -> p k b c", k=2, b=B)
            chained(dve.tensor_scalar(gsgn[:, :, :, :], gps, 0.0, 2.0, ALU.is_ge, ALU.mult))
            chained(dve.tensor_scalar(gsgn[:, :, :, :], gsgn[:, :, :, :], -1.0, None, ALU.add))
            chained(dve.tensor_tensor(gabs[:, :, :, :], gps, gsgn[:, :, :, :], ALU.mult))
            chained(dve.scalar_tensor_tensor(out=gB[:, :, :, :], in0=gabs[:, :, :, :], scalar=0.25,
                                             in1=gsgn[:, :, :, :], op0=ALU.max, op1=ALU.mult))
            for b in range(B):
                ins = dve.tensor_tensor(wog[:, b, :], wo_sb[:, :], gB[:, 0, b, :], ALU.mult)
            ins.then_inc(s["wog_ready"], 1)

            def residue(n):
                b, kq, half = QK[n]
                dve.wait_ge(s["hi_ready"], n + 1)
                if n >= 2:
                    dve.wait_ge(s["lo_ready"], n - 1)
                dve.tensor_tensor(r1[:, n % 2, :], qk_bank[n % 3],
                                  parts[:, kq, 0, b * S + 512 * half:b * S + 512 * half + 512],
                                  ALU.subtract).then_inc(s["r1_ready"], 1)

            for n in range(4):
                residue(n)
            dve.wait_ge(x_in[1], 16)
            aggregate(list(range(8, 16)), s["var_ready"])
            rstd(slice(8, 16), (s["std_ready"], 2))
            for n in range(8, 16):
                normalise(n, s["xn_ready"])
            for n in range(4, 8):
                residue(n)

            def bank(a):
                return aux[:, a % 2, :]

            def max_unit(k, a, par, p):
                h, i, k0, w, diagonal, place = MAXU[k]
                src = bank(par)[:, 0:w]
                at = mxp[:, p, 8 * h + i, place:place + 1]
                dve.wait_ge(s["aux_ready"], a + 1)
                if diagonal:
                    dve.sem_inc(s["passed_v"], 1)
                    ins = dve.tensor_tensor_reduce(src, src, slab[:, 512 - w:512], 1.0, LOWEST, ALU.add, ALU.max, at)
                else:
                    ins = dve.tensor_reduce(at, src, AX_X, ALU.max)
                ins.then_inc(s["aux_free"], 1)

            def maxima(p, a):
                dve.wait_ge(s["aux_free"], a)
                dve.tensor_reduce(negm[:, :], mxp[:, p, :, :], AX_X, ALU.max, negate=True).then_inc(s["negm_ready"], 1)

            def neg_out(a, par):
                dve.wait_ge(s["aux_ready"], a + 1)
                dve.tensor_copy(negT[:, :], bank(par)[0:96, 0:64].bitcast(BF16)).then_inc(s["aux_free"], 1)

            def attn_out(u, p, c, a, par, v):
                dve.wait_ge(s["aux_ready"], a + 1)
                ps = bank(par).rearrange("p (i h c) -> p i h c", i=4, h=HQ)
                dve.reciprocal(rden[:, c, :, :], ps[:, :, :, DK]).then_inc(s["chain_v"], 1)
                dve.wait_ge(s["chain_v"], v + 1)
                dst = attn[:, 8 * p + 4 * c:8 * p + 4 * c + 4, bass.ds(HQ * DK * u, HQ * DK)]
                dve.tensor_tensor(dst.rearrange("p i (h c) -> p i h c", h=HQ), ps[:, :, :, 0:DK],
                                  rden[:, c, :, :].unsqueeze(3).broadcast_to([P, 4, HQ, DK]),
                                  ALU.mult).then_inc(s["aux_free"], 1)

            dve.wait_ge(s["const_ready"], 5)
            for k in range(NM):
                max_unit(k, k, k, 0)
            maxima(0, NM)
            for k in range(FIRST):
                max_unit(k, NM + k, NM + k, 1)
            neg_out(NM + FIRST, NM + FIRST)
            for k in range(FIRST, NM // 2):
                max_unit(k, NM + 1 + k, NM + 1 + k, 1)
            base = link[0]

            def body(t, u, p, plan):
                a = 0
                a0 = AUX0 + AUXN * t
                par = AUX0 + AUXN * p
                for q in TURN:
                    for kind, k, unit in [x for step in plan[q] for x in step]:
                        if kind == "max":
                            max_unit(unit, a0 + a, par + a, (p + k) % 2)
                        elif kind == "turn":
                            dve.wait_ge(s["negrow"], 16 * t + 16)
                            neg_out(a0 + a, par + a)
                        else:
                            attn_out(u, p, k, a0 + a, par + a, base + 2 * t + k)
                        a += 1
                    if q == 2:
                        dve.wait_ge(s["neg3_ready"], t + 1)
                        maxima(1 - p, a0 + a)
                return a

            with dve.Fori(0, T // 2 - 1) as u:
                for p in range(2):
                    body(2 * u + p, u, p, FULL)
            a = AUX0 + AUXN * (T - 2) + body(T - 2, T // 2 - 1, 0, NOT_AHEAD)
            for c in range(2):
                attn_out(T // 2 - 1, 1, c, a + c, a + c, base + 2 * (T - 1) + c)
            link[0] = base + 2 * T

            for g in range(4):
                dve.wait_ge(s["pj_ready"], g + 1)
                ins = dve.tensor_tensor(x_sb[:, 4 * g:4 * g + 4, :], oacc[:, g % 2, :].rearrange("p (n c) -> p n c", n=4),
                                        x_sb[:, 4 * g:4 * g + 4, :], ALU.add)
                ins.then_inc(s["x2_done"], 1)
            dve.wait_ge(s["x2_done"], 4)
            aggregate(list(range(NT)), s["var2_ready"])
            rstd(slice(0, NT), (s["std2_ready"], 1))
            for n in range(NT):
                normalise(n, s["xn2_ready"])
            dve.wait_ge(s["rowmod_ready"], 1)
            dve.wait_ge(s["xn2_ready"], NT)
            mod = aux[:, 0, :].rearrange("p (k b c) -> p k b c", k=2, b=B)
            for b in range(B):
                tiles = slice(8 * b, 8 * b + 8)
                chained(dve.scalar_tensor_tensor(out=rows[:, tiles, :],
                                                 in0=mod[:, 1, b:b + 1, :].broadcast_to([P, 8, C]), scalar=1.0,
                                                 in1=xn[:, tiles, :], op0=ALU.add, op1=ALU.mult))
                ins = dve.tensor_tensor(rows[:, tiles, :], rows[:, tiles, :],
                                        mod[:, 0, b:b + 1, :].broadcast_to([P, 8, C]), ALU.add)
            ins.then_inc(s["h2_ready"], 1)
            dve.wait_ge(s["lg_ready"], 4)
            chained(dve.tensor_copy(lg[:, :, :], aux[:, 1, 0:NT * NE].rearrange("p (n e) -> p n e", e=NE)))
            chained(dve.tensor_reduce(gmx[:, :], lg[:, :, :], AX_X, ALU.max))
            dve.tensor_tensor(lg[:, :, :], lg[:, :, :], gmx[:, :].unsqueeze(2).broadcast_to([P, NT, NE]),
                              ALU.subtract).then_inc(s["ge_ready"], 1)
            dve.wait_ge(s["gx_ready"], 1)
            chained(dve.tensor_reduce(gsm[:, :], gt[:, :, :], AX_X, ALU.add))
            chained(dve.reciprocal(gsm[:, :], gsm[:, :]))
            chained(dve.tensor_tensor(gt[:, :, :], gt[:, :, :], gsm[:, :].unsqueeze(2).broadcast_to([P, NT, NE]),
                                      ALU.mult))
            for n in range(NT):
                ins = dve.max(top[:, n, :], gt[:, n, :])
            chained(ins)
            for n in range(NT):
                ins = dve.max_index(topi[:, n, :], top[:, n, :], gt[:, n, :])
            chained(ins)
            dve.tensor_tensor(tw[:, :, 0], top[:, :, 1], top[:, :, 0], ALU.subtract).then_inc(s["ge_ready"], 1)
            chained(dve.tensor_copy(topf[:, :, :], topi[:, :, 0:2]))
            io = iota8[:, :].unsqueeze(1).broadcast_to([P, NT, NE])
            sel = (lg, gt)
            for k in range(2):
                chained(dve.tensor_tensor(sel[k][:, :, :], io, topf[:, :, k:k + 1].broadcast_to([P, NT, NE]), ALU.is_equal))
            dve.tensor_tensor(chosen[:, NE:].rearrange("p (n e) -> p n e", e=NE), lg[:, :, :], gt[:, :, :],
                              ALU.add).then_inc(s["chosen_ready"], 1)
            dve.wait_ge(s["gx_ready"], 2)
            chained(dve.tensor_scalar(tw[:, :, 0], tw[:, :, 1], 1.0, None, ALU.add))
            chained(dve.reciprocal(tw[:, :, 0], tw[:, :, 0]))
            chained(dve.tensor_tensor(tw[:, :, 1], tw[:, :, 1], tw[:, :, 0], ALU.mult))
            for k in range(2):
                dst = wsel[:, :, :] if k else wgt[:, :, 0:NE]
                chained(dve.tensor_tensor(dst, sel[k][:, :, :], tw[:, :, k:k + 1].broadcast_to([P, NT, NE]), ALU.mult))
            dve.tensor_tensor(wgt[:, :, 0:NE], wgt[:, :, 0:NE], wsel[:, :, :], ALU.add).then_inc(s["wgt_ready"], 1)
            def wt_out(g):
                dve.wait_ge(s["wt_ready"], g + 1)
                dve.tensor_copy(wT[:, 512 * g:512 * g + 512], aux[0:NE + 1, g % 2, :]).then_inc(s["wT_ready"], 1)

            dve.wait_ge(s["prefix_ready"], 1)
            pfx = aux[:, 1, 0:(NT + 1) * NE].rearrange("p (n e) -> p n e", e=NE)
            chained(dve.tensor_tensor(isgt[:, :, :], pfx[:, NT, :].unsqueeze(2).broadcast_to([P, NE, NT]),
                                      thr[:, :].unsqueeze(1).broadcast_to([P, NE, NT]), ALU.is_gt))
            chained(dve.tensor_reduce(tiles_e[:, :], isgt[:, :, :], AX_X, ALU.add))
            chained(dve.tensor_tensor(before[:, :, :], tiles_e[:, :].unsqueeze(1).broadcast_to([P, NE, NE]),
                                      lower[:, :, :], ALU.mult))
            chained(dve.tensor_reduce(base_e[:, :], before[:, :, :], AX_X, ALU.add))
            chained(dve.tensor_tensor(ends_e[:, :], base_e[:, :], tiles_e[:, :], ALU.add))
            chained(dve.tensor_scalar(base_e[:, :], base_e[:, :], float(P), None, ALU.mult))
            chained(dve.tensor_tensor(place[:, :, :], pfx[:, 0:NT, :],
                                      base_e[:, :].unsqueeze(1).broadcast_to([P, NT, NE]), ALU.add))
            for k in range(2):
                chained(dve.tensor_tensor(place1[:, :, :], place[:, :, :], sel[k][:, :, :], ALU.mult))
                chained(dve.tensor_reduce(posf[:, k, :], place1[:, :, :], AX_X, ALU.add))
            chained(dve.tensor_copy(posi[:, :, :], posf[:, :, :]))
            chained(dve.tensor_scalar(posm[:, :, :], posi[:, :, :], P - 1, None, ALU.bitwise_and))
            chained(dve.tensor_copy(posb[:, :, :], posm[:, :, :]))
            chained(dve.tensor_tensor(posa[:, :, :], posf[:, :, :], posb[:, :, :], ALU.subtract))
            chained(dve.tensor_scalar(posa[:, :, :], posa[:, :, :], 1.0 / P, None, ALU.mult))
            wt_out(0)
            dve.tensor_tensor(tiled, num[:, 0:ROUTED].unsqueeze(1).unsqueeze(1).broadcast_to([P, 2, NT, ROUTED]),
                              posa[:, :, :].unsqueeze(3).broadcast_to([P, 2, NT, ROUTED]),
                              ALU.is_equal).then_inc(s["tiled_ready"], 1)
            for k in range(2):
                dve.tensor_tensor(onehot[:, k], num[:, :].unsqueeze(1).broadcast_to([P, NT, P]),
                                  posb[:, k, :].unsqueeze(2).broadcast_to([P, NT, P]),
                                  ALU.is_equal).then_inc(s["onehot_ready"], 1)
            chained(dve.tensor_tensor(past, num[:, 0:ROUTED].unsqueeze(2).broadcast_to([P, ROUTED, NE]),
                                      ends_e[:, :].unsqueeze(1).broadcast_to([P, ROUTED, NE]), ALU.is_ge))
            chained(dve.tensor_reduce(tile_e[:, :], past, AX_X, ALU.add))
            chained(dve.tensor_scalar(tile_e[:, :], tile_e[:, :], float(NE - 1), None, ALU.min))
            dve.tensor_copy(tile_i[:, :], tile_e[:, :]).then_inc(s["te_ready"], 1)
            def down_bank(c):
                return oacc[:, c % 2, :].rearrange("p (n c) -> p n c", n=4)

            def shared_out(c, before, done):
                dve.wait_ge(s["dn_ready"], before + 1)
                gate = gB[:, 1, c // 2:c // 2 + 1, :].broadcast_to([P, 4, C])
                tiles = slice(4 * c, 4 * c + 4)
                dve.tensor_tensor(acc[:, tiles, :], down_bank(c), gate, ALU.mult).then_inc(s["acc_done"], 1)
                dve.wait_ge(s["acc_done"], done + 1)
                dve.tensor_tensor(acc[:, tiles, :], acc[:, tiles, :], x_sb[:, tiles, :], ALU.add)

            shared_out(0, 0, 0)
            dve.wait_ge(s["inv_sum"], 1)
            chained(dve.tensor_scalar(invn[:, :], aux[:, 1, ROUTED:2 * ROUTED], float(P), None, ALU.mult))
            dve.tensor_tensor(inv[:, :], invn[:, :], aux[:, 1, 0:ROUTED], ALU.add).then_inc(s["inv_ready"], 1)
            for g in range(1, 4):
                wt_out(g)
            shared_out(1, 1, 1)
            dve.wait_ge(s["te_ready"], 1)

            def x_copy(i, j):
                dve.wait_ge(s["xt_ready"], FREE + i + 1)
                dve.tensor_copy(xTg[:, j % 2, :], aux[:, j % 2, 0:P]).then_inc(s["xt_done"], 1)

            def up_copy(i, j):
                e = dve.value_load(tile_i[0:1, bass.ds(i, 1)], min_val=0, max_val=NE - 1)
                if not isinstance(i, int) or i >= 2:
                    dve.wait_ge(s["up_ready"], NF * FIRST_STEPS + i - 1)
                    dve.wait_ge(s["silu_done"], NF * FIRST_STEPS + i - 3)
                dve.tensor_copy(wcur[:, j % 2:j % 2 + 1, 0:FF], weights[:, bass.ds(e, 1), 0:FF])
                dve.tensor_copy(bcur[:, j % FREE, :], b1_sb[:, bass.ds(e * NF, NF)]).then_inc(s["up_w"], 1)
                return e

            def down_copy(i, j, e):
                if e is None:
                    e = dve.value_load(tile_i[0:1, bass.ds(i, 1)], min_val=0, max_val=NE - 1)
                if not isinstance(i, int) or i >= 2:
                    dve.wait_ge(s["dn_ready"], FIRST_STEPS + i - 1)
                dve.tensor_copy(wcur[:, j % 2:j % 2 + 1, FF:2 * FF],
                                weights[:, bass.ds(e, 1), FF:2 * FF]).then_inc(s["down_w"], 1)

            dve.wait_ge(s["ew_in"], 16 * (NF + 1))
            dve.wait_ge(s["w2_in"], 16 * 9)
            down_copy(0, 0, up_copy(0, 0))
            e = up_copy(1, 1)
            x_copy(0, 0)
            x_copy(1, 1)
            shared_out(2, 2, 2)
            with dve.Fori(0, ROUTED // ROWS - 1) as u:
                e = None
                for j in range(ROWS):
                    i = ROWS * u + j
                    x_copy(i + 2, j + 2)
                    e2 = up_copy(i + 2, j + 2)
                    down_copy(i + 1, j + 1, e)
                    e = e2
            e = None
            for j in range(ROWS):
                i = ROUTED - ROWS + j
                if i + 2 < ROUTED:
                    x_copy(i + 2, j + 2)
                    e2 = up_copy(i + 2, j + 2)
                if i + 1 < ROUTED:
                    down_copy(i + 1, j + 1, e)
                    e = e2
            shared_out(3, FIRST_STEPS + ROUTED, 3)
            for g in range(4):
                tiles = slice(4 * g, 4 * g + 4)
                dve.wait_ge(yk_in[g], 16 * 8)
                gate = gB[:, 1, g // 2:g // 2 + 1, :].broadcast_to([P, 4, C])
                for n in range(4 * g, 4 * g + 4):
                    ins = dve.tensor_scalar(yk[:, 0, n, :], yk[:, 0, n, :], tw[:, n, 0:1], None, ALU.mult)
                chained(ins)
                for n in range(4 * g, 4 * g + 4):
                    ins = dve.scalar_tensor_tensor(out=yk[:, 0, n, :], in0=yk[:, 1, n, :], scalar=tw[:, n, 1:2],
                                                   in1=yk[:, 0, n, :], op0=ALU.mult, op1=ALU.add)
                chained(ins)
                chained(dve.tensor_tensor(yk[:, 0, tiles, :], yk[:, 0, tiles, :], gate, ALU.mult))
                dve.tensor_tensor(yout[:, tiles, :], yk[:, 0, tiles, :], acc[:, tiles, :], ALU.add).then_inc(s["y_ready"], 1)

        @block.tensor
        def _(pe):
            pe.sem_inc(s["pv_done"], 1)
            pe.sem_inc(s["out_turned"], 2)
            pe.sem_inc(s["xt_ready"], FREE)
            pe.wait_ge(s["w_in"], 128)
            for k in range(3):
                ins = pe.matmul(aux[:, 0, P * k:P * k + P], wd_sb[:, min(k, 1), :], wu_sb[:, k, :],
                                start=True, stop=True)
            ins.then_inc(s["comp_ready"], 1)
            pe.wait_ge(s["cs_ready"], 1)
            for j in range(6):
                pe.matmul(aux[:, 1, 2 * j:2 * j + 2], wmod_sb[:, C * j:C * j + C], cs[:, :], start=True, stop=True)
            pe.wait_ge(s["csb_ready"], 1)
            for k in range(2):
                for b in range(B):
                    ins = pe.matmul(oacc[:, 0, P * (2 * k + b):P * (2 * k + b) + P], csB[:, b, :],
                                    wmod_sb[:, C * (3 * k + 2):C * (3 * k + 3)], start=True, stop=True)
            ins.then_inc(s["mod_ready"], 1)
            pe.wait_ge(s["const_ready"], 2)

            def x_turn(g):
                if g >= 2:
                    pe.wait_ge(s["hT_ready"], g - 1)
                for i in range(4):
                    n = 4 * g + i
                    pe.wait_ge(s["xn_ready"], n + 1)
                    ins = pe.transpose(sc[:, g % 2, P * i:P * i + P], xn[:, n, :], ident[:, :])
                ins.then_inc(s["xT_ready"], 1)

            def project(n):
                b, kq, half = QK[n]
                pe.wait_ge(s["hT_ready"], 2 * b + half + 1)
                if n >= 3:
                    pe.wait_ge(s["r1_ready"], n - 2)
                pe.matmul(qk_bank[n % 3], wqkv[:, 1 - kq, :], hT[:, b * S + 512 * half:b * S + 512 * half + 512],
                          start=True, stop=True).then_inc(s["qk_ready"], 1)

            def project_v(g):
                if g >= 2:
                    pe.wait_ge(s["v_done"], g - 1)
                elif g == 1:
                    pe.wait_ge(s["mod_done"], 1)
                for i in range(4):
                    n = 4 * g + i
                    ins = pe.matmul(aux[:, g % 2, P * i:P * i + P], hT[:, P * n:P * n + P], wqkv[:, 2, :],
                                    start=True, stop=True)
                ins.then_inc(s["v_ready"], 1)

            x_turn(0)
            x_turn(1)
            pe.wait_ge(s["wqkv_ready"], 1)
            for n in range(4):
                project(n)
            project_v(0)
            project_v(1)
            x_turn(2)
            x_turn(3)
            for n in range(4, 8):
                project(n)
            project_v(2)
            project_v(3)

            def max_scores(k, a, par, p):
                h, i, k0, w, diagonal, place = MAXU[k]
                if not isinstance(a, int) or a >= 2:
                    pe.wait_ge(s["aux_free"], a - 1)
                pe.matmul(aux[:, par % 2, 0:w], S1[0:CROSS, p, 1, S * h + P * i:S * h + P * i + P],
                          S1[0:CROSS, p, 0, S * h + k0:S * h + k0 + w], start=True, stop=True).then_inc(s["aux_ready"], 1)

            def turn_max(a, par, n):
                pe.wait_ge(s["neg3_ready"], n)
                pe.wait_ge(s["aux_free"], a - 1)
                pe.transpose(aux[0:96, par % 2, 0:64].bitcast(BF16), neg3[:, :, :].rearrange("p a c -> p (a c)"),
                             identb[:, :]).then_inc(s["aux_ready"], 1)

            def score_unit(t, slot, n, p):
                j, h0, nh, w, pitch = UNITS[slot][n]
                g = NU * t + UBASE[slot] + n
                if not isinstance(g, int) or g >= 2:
                    pe.wait_ge(s["exp_done"], g - 1)
                if slot == 0 and n == 0:
                    pe.wait_ge(s["negrow"], 16 * t + 16)
                buf = (UBASE[slot] + n) % 2
                dst = sc[:, 2 * buf:2 * buf + 2, :].rearrange("p a c -> p (a c)")
                for k in range(nh):
                    h = h0 + k
                    for c in range(0, w, 512):
                        m = min(512, w - c)
                        q = S * h + P * j + c
                        pe.matmul(dst[:, pitch * k + c:pitch * k + c + m],
                                  S2[0:NEG_ROW + 3, p, 0, S * h + P * j:S * h + P * j + P],
                                  S2[0:NEG_ROW + 3, p, 1, q:q + m], start=True, stop=True)
                    ins = pe.matmul(dst[:, pitch * k:pitch * k + P], identb[:, :], after[:, :],
                                    start=False, stop=True, skip_group_check=True)
                ins.then_inc(s["score_ready"], 1)

            def weigh(t, slot, c, p):
                j = SLOTS[slot]
                q0 = max(512 * c, P * j)
                if c == 0 or slot % 2:
                    pe.wait_ge(s["exp_done"], NU * t + UBASE[slot + 1])
                if slot == 0 and c == 0:
                    pe.wait_ge(s["vb_ready"], t + 1)
                    pe.wait_ge(s["o_done"], 2 * t + 1)
                for h in range(HQ):
                    if slot % 2:
                        src = prs[:, h, q0 - 512:512]
                    else:
                        src = pr[:, slot // 2 % 2, h, q0:512 * c + 512]
                    ins = pe.matmul(oacc[VW * h:VW * h + VW, c, q0 - 512 * c:512], vb[:, p, j, h, :], src,
                                    start=(slot == 0), stop=(slot == (6 if c == 0 else 7)))
                if c == 1:
                    ins.then_inc(s["pv_done"], 1)

            def turn_out(t, c, a, par):
                pe.wait_ge(s["o_done"], 2 * t + c + 2)
                pe.wait_ge(s["aux_free"], a - 1)
                for i in range(4):
                    ins = pe.transpose(aux[:, par % 2, P * i:P * i + P], osb[:, c, P * i:P * i + P], ident[:, :])
                ins.then_inc(s["aux_ready"], 1)
                pe.sem_inc(s["out_turned"], 1)

            def weigh_pair(t, q, p, step):
                if step < 2:
                    weigh(t, 2 * q, step, p)
                if step == 1:
                    weigh(t, 2 * q + 1, 1, p)

            def body(t, u, p, plan, more):
                a = 0
                a0 = AUX0 + AUXN * t
                par = AUX0 + AUXN * p
                for q in TURN if more else (1, 2, 3):
                    at = (t + 1, 1 - p) if q == 0 else (t, p)
                    if q == 0:
                        pe.wait_ge(s2_in[1 - p], 32 * (u + p + 1))
                    if q == 3 and plan is FULL:
                        pe.wait_ge(s1_in[p], 16 * NLOAD * (u + 2))
                    for step, (slot, n) in enumerate(pair_steps(q)):
                        score_unit(at[0], slot, n, at[1])
                        units = plan[q][step] if plan else []
                        if len(units) < BEFORE:
                            weigh_pair(t, (q - 1) % 4, p, step)
                        for n, (kind, k, unit) in enumerate(units):
                            if n == BEFORE:
                                weigh_pair(t, (q - 1) % 4, p, step)
                            if kind == "max":
                                max_scores(unit, a0 + a, par + a, (p + k) % 2)
                            elif kind == "turn":
                                turn_max(a0 + a, par + a, t + 2)
                            else:
                                turn_out(t, k, a0 + a, par + a)
                            a += 1
                        if len(units) == BEFORE:
                            weigh_pair(t, (q - 1) % 4, p, step)
                return a

            pe.wait_ge(s["v_done"], 4)
            pe.wait_ge(s1_in[0], 16 * NLOAD)
            for k in range(NM):
                max_scores(k, k, k, 0)
            pe.wait_ge(s1_in[1], 16 * NLOAD)
            for k in range(FIRST):
                max_scores(k, NM + k, NM + k, 1)
            turn_max(NM + FIRST, NM + FIRST, 1)
            for k in range(FIRST, NM // 4):
                max_scores(k, NM + 1 + k, NM + 1 + k, 1)
            pe.wait_ge(s2_in[0], 32)
            pe.wait_ge(s["r1_ready"], 8)
            steps = len(pair_steps(0))
            for step, (slot, n) in enumerate(pair_steps(0)):
                score_unit(0, slot, n, 0)
                for k in range(NM // 4 + NM // 4 * step // steps, NM // 4 + NM // 4 * (step + 1) // steps):
                    max_scores(k, NM + 1 + k, NM + 1 + k, 1)
            with pe.Fori(0, T // 2 - 1) as u:
                for p in range(2):
                    body(2 * u + p, u, p, FULL, True)
            a = AUX0 + AUXN * (T - 2) + body(T - 2, T // 2 - 1, 0, NOT_AHEAD, True)
            body(T - 1, T // 2 - 1, 1, None, False)
            for step in range(2):
                weigh_pair(T - 1, 3, 1, step)
            for c in range(2):
                turn_out(T - 1, c, a + c, a + c)

            pe.wait_ge(s["exp_done"], NU * T)
            pe.wait_ge(s["aux_free"], a + 2)
            pe.wait_ge(s["wog_ready"], 1)
            for k in range(2):
                for b in range(B):
                    ins = pe.matmul(aux[:, 0, P * (2 * k + b):P * (2 * k + b) + P], csB[:, b, :],
                                    wmod_sb[:, C * (3 + k):C * (4 + k)], start=True, stop=True)
            ins.then_inc(s["rowmod_ready"], 1)
            for g in range(5):
                if g < 4:
                    for i in range(4):
                        n = 4 * g + i
                        ins = pe.transpose(sc[:, g, P * i:P * i + P], attn[:, n, :],
                                           ident[:, :])
                    ins.then_inc(s["at_ready"], 1)
                if g:
                    k = g - 1
                    pe.wait_ge(s["at_done"], k + 1)
                    if k >= 2:
                        pe.wait_ge(s["x2_done"], k - 1)
                    else:
                        pe.wait_ge(s["o_done"], 2 * T + 1)
                    for i in range(4):
                        ins = pe.matmul(oacc[:, k % 2, P * i:P * i + P], aT[:, k % 2, P * i:P * i + P], wog[:, k // 2, :],
                                        start=True, stop=True)
                    ins.then_inc(s["pj_ready"], 1)
            pe.wait_ge(s["w2_in"], 16 * 9)
            for g in range(4):
                for i in range(4):
                    n = 4 * g + i
                    pe.wait_ge(s["xn2_ready"], n + 1)
                    ins = pe.transpose(sc[:, g, P * i:P * i + P], xn[:, n, :], ident[:, :])
                ins.then_inc(s["x2T_ready"], 1)
            for g in range(4):
                pe.wait_ge(s["h2T_ready"], g + 1)
                if g >= 2:
                    pe.wait_ge(s["r1T_ready"], g - 1)
                pe.matmul(oacc[0:32, g % 2, :], wr1_sb[:, :], h2T[:, 512 * g:512 * g + 512],
                          start=True, stop=True).then_inc(s["rt_ready"], 1)
            for g in range(4):
                pe.wait_ge(s["r1T_ready"], g + 1)
                for i in range(4):
                    n = 4 * g + i
                    ins = pe.matmul(aux[:, 1, NE * n:NE * n + NE], r1T[:, P * n:P * n + P], wr2_sb[:, :],
                                    start=True, stop=True)
                ins.then_inc(s["lg_ready"], 1)

            def up(k, c, w, silus=None):
                for f in range(NF):
                    if silus is not None:
                        pe.wait_ge(s["silu_done"], silus)
                    elif k >= 1:
                        pe.wait_ge(s["silu_done"], NF * k + f - NF + 1)
                    pe.matmul(sc[:, f, :], w[:, P * f:P * f + P], h2T[:, 512 * c:512 * c + 512],
                              start=True, stop=True).then_inc(s["up_ready"], 1)

            def down(k, c, w, silus=None):
                pe.wait_ge(s["silu_done"], (NF * k if silus is None else silus) + NF)
                if silus is not None:
                    pe.wait_ge(s["y_done"], ROUTED + 2)
                elif k >= 2:
                    pe.wait_ge(s["acc_done"], k - 1)
                for i in range(4):
                    n = 4 * c + i
                    dst = oacc[:, c % 2, P * i:P * i + P]
                    pe.matmul(dst, wT[:, P * n:P * n + P], be2_sb[:, :], start=True, stop=False)
                    for f in range(NF):
                        ins = pe.matmul(dst, sT[:, c % 2, f, P * i:P * i + P], w[:, f, :],
                                        start=False, stop=(f == NF - 1))
                ins.then_inc(s["dn_ready"], 1)

            up(0, 0, sh_up[:, :])
            pe.wait_ge(s["chosen_ready"], 1)
            pfx = aux[:, 1, 0:(NT + 1) * NE]
            pe.matmul(pfx, ones[:, :], chosen[:, :], start=True, stop=True)
            pe.matmul(pfx[:, 0:NT * NE], upper[:, :], chosen[:, NE:], start=False, stop=True, skip_group_check=True)
            for d in range(2, NT + 1):
                ins = pe.matmul(pfx[:, NE * d:], ones[:, :], chosen[:, NE:NE * (NT + 2 - d)], start=False,
                                stop=True, skip_group_check=True)
            ins.then_inc(s["prefix_ready"], 1)
            up(1, 1, sh_up[:, :])
            def turn_gates(g):
                if g >= 2:
                    pe.wait_ge(s["wT_ready"], g - 1)
                for i in range(4):
                    n = 4 * g + i
                    ins = pe.transpose(aux[0:NE + 1, g % 2, P * i:P * i + P], wgt[:, n, :], ident[:, :])
                ins.then_inc(s["wt_ready"], 1)

            pe.wait_ge(s["wgt_ready"], 1)
            pe.wait_ge(s["h2_ready"], 1)
            turn_gates(0)
            pe.wait_ge(s["wT_ready"], 1)
            down(0, 0, sh_dn[:, :, :])
            up(2, 2, sh_up[:, :])
            pe.wait_ge(s["tiled_ready"], 3)
            for k in range(2):
                pe.wait_ge(s["onehot_ready"], k + 1)
                for n in range(NT):
                    ins = pe.matmul(aux[:, 1, 0:2 * ROUTED].rearrange("p (q a) -> p q a", q=2), onehot[:, k, n, :],
                                    tiledpn[:, :, k, n, :], start=(k == 0 and n == 0), stop=(k == 1 and n == NT - 1))
            ins.then_inc(s["inv_sum"], 1)
            pe.wait_ge(s["inv_ready"], 1)
            for g in range(1, 4):
                turn_gates(g)
            pe.wait_ge(s["wT_ready"], 2)
            down(1, 1, sh_dn[:, :, :])

            def turn_rows(i, j, u):
                pe.wait_ge(rows_in[j % FREE], 16 * (ROWS // FREE * u + j // FREE) + 16)
                if not isinstance(i, int) or i >= 2:
                    pe.wait_ge(s["xt_done"], i - 1)
                pe.transpose(aux[:, j % 2, 0:P], xrow[:, j % FREE, :], ident[:, :]).then_inc(s["xt_ready"], 1)

            def up_tile(i, j):
                pe.wait_ge(s["xt_done"], i + 1)
                pe.wait_ge(s["up_w"], i + 1)
                pe.wait_ge(s["silu_done"], NF * FIRST_STEPS + i - 1)
                for f in range(NF):
                    ins = pe.matmul(sc[:, j % 2, P * f:P * f + P], wcur[:, j % 2, P * f:P * f + P], xTg[:, j % 2, :],
                                    start=True, stop=True)
                ins.then_inc(s["up_ready"], 1)

            def down_tile(i, j):
                pe.wait_ge(s["silu_done"], NF * FIRST_STEPS + i + 1)
                pe.wait_ge(s["down_w"], i + 1)
                if j < 2:
                    pe.wait_ge(s["acc_done"], FIRST_STEPS)
                pe.wait_ge(s["y_done"], i + 1)
                for f in range(NF):
                    ins = pe.matmul(oacc[:, j % 2, 0:P], hid[:, j % 2, P * f:P * f + P],
                                    wcur[:, j % 2, FF + C * f:FF + C * f + C], start=(f == 0), stop=(f == NF - 1))
                ins.then_inc(s["dn_ready"], 1)

            pe.wait_ge(s["wT_ready"], 4)
            turn_rows(0, 0, 0)
            turn_rows(1, 1, 0)
            up_tile(0, 0)
            down(2, 2, sh_dn[:, :, :])
            with pe.Fori(0, ROUTED // ROWS - 1) as u:
                for j in range(ROWS):
                    i = ROWS * u + j
                    turn_rows(i + 2, j + 2, u)
                    up_tile(i + 1, j + 1)
                    down_tile(i, j)
            for j in range(ROWS):
                i = ROUTED - ROWS + j
                if i + 2 < ROUTED:
                    turn_rows(i + 2, j + 2, ROUTED // ROWS - 1)
                if i + 1 < ROUTED:
                    up_tile(i + 1, j + 1)
                down_tile(i, j)
            up(3, 3, sh_up[:, :], silus=NF * FIRST_STEPS + ROUTED)
            down(3, 3, sh_dn[:, :, :], silus=NF * FIRST_STEPS + ROUTED)


def kernel(**inputs):
    import numpy as _np
    import concourse.bacc as _bacc
    from concourse import mybir as _mybir
    from concourse.bass_utils import run_bass_kernel_spmd as _run

    a = {k.replace("L0_", ""): _np.asarray(v) for k, v in inputs.items()}
    row = lambda v: v.reshape(1, -1)
    NE, F = a["ffn_be1"].shape
    biases = _np.concatenate([a["ffn_be1"], row(a["ffn_bs1"])], 0).reshape(NE + 1, F // 128, 128)
    data = {
        "x": a["attn_x"], "cT": a["c"].T, "wmod": a["wmod"], "wdqT": a["attn_W_dq"].T, "wdkvT": a["attn_W_dkv"].T,
        "wuq": a["attn_W_uq"], "wuk": a["attn_W_uk"], "wuv": a["attn_W_uv"], "wo": a["attn_W_o"],
        "wr1": a["ffn_Wr1"], "br1": a["ffn_br1"].reshape(-1, 1), "wr2": a["ffn_Wr2"], "br2": row(a["ffn_br2"]),
        "ws1": a["ffn_Ws1"], "ws2": a["ffn_Ws2"], "bs2": row(a["ffn_bs2"]), "we1": a["ffn_We1"], "we2": a["ffn_We2"],
        "be2": a["ffn_be2"], "b1T": biases.transpose(2, 0, 1).reshape(128, -1),
    }
    nc = _bacc.Bacc("TRN2", target_bir_lowering=False, num_devices=1)
    arrays, args = {}, []
    for name, v in data.items():
        v = _np.ascontiguousarray(v)
        arrays[f"in_{name}"] = v
        args.append(nc.dram_tensor(f"in_{name}", v.shape, _mybir.dt.from_np(v.dtype), kind="ExternalInput").ap())
    out = nc.dram_tensor("out_y", a["attn_x"].shape, _mybir.dt.float32, kind="ExternalOutput").ap()
    adaln_layer(nc, *args, out)
    r = _run(nc, [arrays], core_ids=[0])
    return r.results[0]["out_y"]
```
